# Optimizing a Trainium2 kernel written in Bass

```python
import numpy as np
import jax
import jax.numpy as jnp

def _softmax(x, axis=-1):
    return jax.nn.softmax(x, axis=axis)

def _gelu(x):
    return jax.nn.gelu(x, approximate=True)

def _silu(x):
    return jax.nn.silu(x)

def _sigmoid(x):
    return jax.nn.sigmoid(x)

def _layernorm(x, axis=-1, eps=1e-05):
    m = jnp.mean(x, axis=axis, keepdims=True)
    v = jnp.var(x, axis=axis, keepdims=True)
    return (x - m) / jnp.sqrt(v + eps)

def _scatter_add(tgt, idx, src, axis=0):
    return tgt.at[idx].add(src)

def _segment_sum(src, seg, n):
    return jax.ops.segment_sum(src, seg, n)
kernel_name = 'mk_vit_tower_d1_tok_img768_r4_9559c4'

def setup_inputs(seed: int=0):
    np.random.seed(seed)
    _w = jnp.asarray

    def _rec_inputs():
        import jax
        import jax.numpy as jnp
        _rk = jax.random.key(seed)
        x = -0.000125008 + 0.999885 * jax.random.normal(jax.random.fold_in(_rk, 1), (64, 4, 96, 96), jnp.float32)
        return x
    x = _rec_inputs()

    def _L0_tok_setup():
        import jax, jax.numpy as jnp
        import numpy as np
        P = 32
        C = 4
        PATCH_DIM = C * P * P
        HIDDEN = 192
        EPS = 1e-05

        def _layernorm(x, gamma, beta):
            mu = jnp.mean(x, axis=-1, keepdims=True)
            var = jnp.mean(jnp.square(x - mu), axis=-1, keepdims=True)
            return (x - mu) * jax.lax.rsqrt(var + EPS) * gamma + beta
        key = jax.random.key(seed)
        ks = jax.random.split(key, 6)
        B, H, W = (32, 128, 128)
        x = jax.random.normal(ks[0], (B, C, H, W), dtype=jnp.float32)
        ln1_g = jnp.ones((PATCH_DIM,), jnp.float32)
        ln1_b = jnp.zeros((PATCH_DIM,), jnp.float32)
        W_proj = jax.random.normal(ks[1], (PATCH_DIM, HIDDEN), jnp.float32) / np.sqrt(PATCH_DIM)
        b_proj = jnp.zeros((HIDDEN,), jnp.float32)
        ln2_g = jnp.ones((HIDDEN,), jnp.float32)
        ln2_b = jnp.zeros((HIDDEN,), jnp.float32)
        return {'x': x, 'ln1_g': ln1_g, 'ln1_b': ln1_b, 'W_proj': W_proj, 'b_proj': b_proj, 'ln2_g': ln2_g, 'ln2_b': ln2_b}
    _L0_tok_all = _L0_tok_setup()
    _L0_tok_in = {k: v for k, v in _L0_tok_all.items() if k in ('ln1_g', 'ln1_b', 'W_proj', 'b_proj', 'ln2_g', 'ln2_b')}
    del _L0_tok_all

    def _L0_attn_setup():
        import jax, jax.numpy as jnp
        import numpy as np
        H = 12

        def _attn(q, k, v):
            D = q.shape[-1]
            scores = jnp.einsum('bhnd,bhmd->bhnm', q, k) / jnp.sqrt(jnp.asarray(D, q.dtype))
            p = jax.nn.softmax(scores, axis=-1)
            return jnp.einsum('bhnm,bhmd->bhnd', p, v)
        key = jax.random.key(seed)
        ks = jax.random.split(key, 5)
        B, N, C = (2, 512, 192)
        s = 0.02
        return {'x': jax.random.normal(ks[0], (B, N, C), jnp.float32), 'Wq': jax.random.normal(ks[1], (C, 2 * C), jnp.float32) * s, 'Wk': jax.random.normal(ks[2], (C, 2 * C), jnp.float32) * s, 'Wv': jax.random.normal(ks[3], (C, C), jnp.float32) * s, 'lambda_p': jnp.zeros((H, 1, 1), jnp.float32), 'Wo': jax.random.normal(ks[4], (C, C), jnp.float32) * s, 'bo': jnp.zeros((C,), jnp.float32)}
    _L0_attn_all = _L0_attn_setup()
    _L0_attn_in = {k: v for k, v in _L0_attn_all.items() if k in ('Wq', 'Wk', 'Wv', 'lambda_p', 'Wo', 'bo')}
    del _L0_attn_all

    def _L0_ffn_setup():
        import math
        import jax, jax.numpy as jnp
        import numpy as np
        EMBED_CHOICES = [96, 144, 192]
        RATIO_CHOICES = [2, 3, 4]
        E_MAX = 192
        H_MAX = 768

        def new_gelu(x):
            c = math.sqrt(2.0 / math.pi)
            return 0.5 * x * (1.0 + jnp.tanh(c * (x + 0.044715 * x * x * x)))

        def _mixed_coeffs(alpha_e, alpha_r):
            h_idx = jnp.arange(H_MAX)
            d_idx = jnp.arange(E_MAX)
            C0 = jnp.zeros((H_MAX, E_MAX), jnp.float32)
            c0b = jnp.zeros((H_MAX,), jnp.float32)
            C1 = jnp.zeros((E_MAX, H_MAX), jnp.float32)
            c1b = jnp.zeros((E_MAX,), jnp.float32)
            for i, e in enumerate(EMBED_CHOICES):
                m_in = (d_idx < e).astype(jnp.float32)
                for j, r in enumerate(RATIO_CHOICES):
                    a = alpha_e[i] * alpha_r[j]
                    m_out = (h_idx < r * e).astype(jnp.float32)
                    C0 = C0 + a * (m_out[:, None] * m_in[None, :])
                    c0b = c0b + a * m_out
                    C1 = C1 + a * (m_in[:, None] * m_out[None, :])
                    c1b = c1b + a * m_in
            return (C0, c0b, C1, c1b)
        key = jax.random.key(seed)
        ks = jax.random.split(key, 6)
        x = jax.random.normal(ks[0], (8, 512, E_MAX), jnp.float32)
        w_fc = jax.random.normal(ks[1], (H_MAX, E_MAX), jnp.float32) * 0.02
        b_fc = jnp.zeros((H_MAX,), jnp.float32)
        w_proj = jax.random.normal(ks[2], (E_MAX, H_MAX), jnp.float32) * 0.02
        b_proj = jnp.zeros((E_MAX,), jnp.float32)
        alpha_e = jax.nn.softmax(jax.random.normal(ks[3], (3,), jnp.float32))
        alpha_r = jax.nn.softmax(jax.random.normal(ks[4], (3,), jnp.float32))
        return {'x': x, 'w_fc': w_fc, 'b_fc': b_fc, 'w_proj': w_proj, 'b_proj': b_proj, 'alpha_e': alpha_e, 'alpha_r': alpha_r}
    _L0_ffn_all = _L0_ffn_setup()
    _L0_ffn_in = {k: v for k, v in _L0_ffn_all.items() if k in ('w_fc', 'b_fc', 'w_proj', 'b_proj', 'alpha_e', 'alpha_r')}
    del _L0_ffn_all
    return {'x': x, 'L0_tok_ln1_g': _L0_tok_in['ln1_g'], 'L0_tok_ln1_b': _L0_tok_in['ln1_b'], 'L0_tok_W_proj': _L0_tok_in['W_proj'], 'L0_tok_b_proj': _L0_tok_in['b_proj'], 'L0_tok_ln2_g': _L0_tok_in['ln2_g'], 'L0_tok_ln2_b': _L0_tok_in['ln2_b'], 'L0_attn_Wq': _L0_attn_in['Wq'], 'L0_attn_Wk': _L0_attn_in['Wk'], 'L0_attn_Wv': _L0_attn_in['Wv'], 'L0_attn_lambda_p': _L0_attn_in['lambda_p'], 'L0_attn_Wo': _L0_attn_in['Wo'], 'L0_attn_bo': _L0_attn_in['bo'], 'L0_ffn_w_fc': _L0_ffn_in['w_fc'], 'L0_ffn_b_fc': _L0_ffn_in['b_fc'], 'L0_ffn_w_proj': _L0_ffn_in['w_proj'], 'L0_ffn_b_proj': _L0_ffn_in['b_proj'], 'L0_ffn_alpha_e': _L0_ffn_in['alpha_e'], 'L0_ffn_alpha_r': _L0_ffn_in['alpha_r']}

def reference(x, L0_tok_ln1_g, L0_tok_ln1_b, L0_tok_W_proj, L0_tok_b_proj, L0_tok_ln2_g, L0_tok_ln2_b, L0_attn_Wq, L0_attn_Wk, L0_attn_Wv, L0_attn_lambda_p, L0_attn_Wo, L0_attn_bo, L0_ffn_w_fc, L0_ffn_b_fc, L0_ffn_w_proj, L0_ffn_b_proj, L0_ffn_alpha_e, L0_ffn_alpha_r):
    import jax
    import jax.numpy as jnp

    def _L0_tok_ref(x, ln1_g, ln1_b, W_proj, b_proj, ln2_g, ln2_b):
        import jax, jax.numpy as jnp
        import numpy as np
        P = 32
        C = 4
        PATCH_DIM = C * P * P
        HIDDEN = 192
        EPS = 1e-05

        def _layernorm(x, gamma, beta):
            mu = jnp.mean(x, axis=-1, keepdims=True)
            var = jnp.mean(jnp.square(x - mu), axis=-1, keepdims=True)
            return (x - mu) * jax.lax.rsqrt(var + EPS) * gamma + beta
        B, c, H, W = x.shape
        h, w = (H // P, W // P)
        patches = x.reshape(B, c, h, P, w, P)
        patches = patches.transpose(0, 2, 4, 3, 5, 1)
        patches = patches.reshape(B, h * w, P * P * c)
        y = _layernorm(patches, ln1_g, ln1_b)
        y = jnp.einsum('bnd,dk->bnk', y, W_proj) + b_proj
        y = _layernorm(y, ln2_g, ln2_b)
        return y

    def _L0_attn_ref(x, Wq, Wk, Wv, lambda_p, Wo, bo):
        import jax, jax.numpy as jnp
        import numpy as np
        H = 12

        def _attn(q, k, v):
            D = q.shape[-1]
            scores = jnp.einsum('bhnd,bhmd->bhnm', q, k) / jnp.sqrt(jnp.asarray(D, q.dtype))
            p = jax.nn.softmax(scores, axis=-1)
            return jnp.einsum('bhnm,bhmd->bhnd', p, v)
        B, N, C = x.shape
        D = C // H
        q = (x @ Wq).reshape(B, N, 2, H, D).transpose(2, 0, 3, 1, 4)
        k = (x @ Wk).reshape(B, N, 2, H, D).transpose(2, 0, 3, 1, 4)
        v = (x @ Wv).reshape(B, N, H, D).transpose(0, 2, 1, 3)
        out1 = _attn(q[0], k[0], v)
        out2 = _attn(q[1], k[1], v)
        lam = jnp.exp(lambda_p)
        out = out1 - lam * out2
        out = out.transpose(0, 2, 1, 3).reshape(B, N, C)
        return out @ Wo + bo

    def _L0_ffn_ref(x, w_fc, b_fc, w_proj, b_proj, alpha_e, alpha_r):
        import math
        import jax, jax.numpy as jnp
        import numpy as np
        EMBED_CHOICES = [96, 144, 192]
        RATIO_CHOICES = [2, 3, 4]
        E_MAX = 192
        H_MAX = 768

        def new_gelu(x):
            c = math.sqrt(2.0 / math.pi)
            return 0.5 * x * (1.0 + jnp.tanh(c * (x + 0.044715 * x * x * x)))

        def _mixed_coeffs(alpha_e, alpha_r):
            h_idx = jnp.arange(H_MAX)
            d_idx = jnp.arange(E_MAX)
            C0 = jnp.zeros((H_MAX, E_MAX), jnp.float32)
            c0b = jnp.zeros((H_MAX,), jnp.float32)
            C1 = jnp.zeros((E_MAX, H_MAX), jnp.float32)
            c1b = jnp.zeros((E_MAX,), jnp.float32)
            for i, e in enumerate(EMBED_CHOICES):
                m_in = (d_idx < e).astype(jnp.float32)
                for j, r in enumerate(RATIO_CHOICES):
                    a = alpha_e[i] * alpha_r[j]
                    m_out = (h_idx < r * e).astype(jnp.float32)
                    C0 = C0 + a * (m_out[:, None] * m_in[None, :])
                    c0b = c0b + a * m_out
                    C1 = C1 + a * (m_in[:, None] * m_out[None, :])
                    c1b = c1b + a * m_in
            return (C0, c0b, C1, c1b)
        C0, c0b, C1, c1b = _mixed_coeffs(alpha_e, alpha_r)
        W0 = w_fc * C0
        b0 = b_fc * c0b
        h = jnp.einsum('bte,he->bth', x, W0) + b0
        h = new_gelu(h)
        W1 = w_proj * C1
        b1 = b_proj * c1b
        out = jnp.einsum('bth,eh->bte', h, W1) + b1
        return out
    h = _L0_tok_ref(x, L0_tok_ln1_g, L0_tok_ln1_b, L0_tok_W_proj, L0_tok_b_proj, L0_tok_ln2_g, L0_tok_ln2_b)
    h = h + _L0_attn_ref(_layernorm(h, axis=-1), L0_attn_Wq, L0_attn_Wk, L0_attn_Wv, L0_attn_lambda_p, L0_attn_Wo, L0_attn_bo)
    h = h + _L0_ffn_ref(_layernorm(h, axis=-1), L0_ffn_w_fc, L0_ffn_b_fc, L0_ffn_w_proj, L0_ffn_b_proj, L0_ffn_alpha_e, L0_ffn_alpha_r)
    return h

_drawn_inputs = setup_inputs


def setup_inputs(seed=0):
    import zlib

    import numpy as np

    out = dict(_drawn_inputs(seed))
    spreads = {'L0_tok_ln1_g': (1.0, 0.2),
     'L0_tok_ln1_b': (0.0, 0.1),
     'L0_tok_b_proj': (0.0, 0.1),
     'L0_tok_ln2_g': (1.0, 0.2),
     'L0_tok_ln2_b': (0.0, 0.1),
     'L0_attn_lambda_p': (0.0, 0.8),
     'L0_attn_bo': (0.0, 0.721),
     'L0_ffn_b_fc': (0.0, 0.436),
     'L0_ffn_b_proj': (0.0, 0.1)}
    factors = {'L0_attn_Wq': 8.0,
     'L0_attn_Wk': 8.0,
     'L0_attn_Wv': 8.0,
     'L0_attn_Wo': 8.0,
     'L0_ffn_alpha_r': 4.849}
    for name, (base, spread) in spreads.items():
        noise = np.random.default_rng([zlib.crc32(name.encode()), seed]).standard_normal(out[name].shape)
        drawn = base * np.exp(spread * noise) if base else spread * noise
        out[name] = jnp.asarray(drawn.astype(out[name].dtype))
    for name, factor in factors.items():
        out[name] = (out[name] * factor).astype(out[name].dtype)
    return out
```

```python
from contextlib import ExitStack

import concourse.bass as bass
from concourse import mybir

F32 = mybir.dt.float32
F32R = mybir.dt.float32r
ALU = mybir.AluOpType
ACT = mybir.ActivationFunctionType
AX_X = mybir.AxisListType.X

P = 128
PATCH = 32
CH = 4
D1 = CH * PATCH * PATCH
HID = 192
EPS = 1e-5
EMBED = (96, 144, 192)
RATIO = (2, 3, 4)
FF = 768


def vit_block(nc, x, ln1_g, ln1_b, W_proj, b_proj, ln2_g, ln2_b, Wq, Wk, Wv, lambda_p, Wo, bo,
              w_fc, b_fc, w_out, b_out, alpha_e, alpha_r, out):
    B, _, IMG, _ = x.shape
    SIDE = IMG // PATCH
    NTOK = SIDE * SIDE
    BH = 32
    HALVES = B // BH
    TILES = HALVES * SIDE
    TT = SIDE * BH
    HEADS = lambda_p.shape[0]
    DH = HID // HEADS
    HQ = P // BH
    HPG = HEADS // HQ
    GW = HPG * DH
    G5 = 5
    KC = 16
    NK = D1 // P
    WC = 8
    NWC = NK // WC
    YW = 2 * HID + 2
    LO = HID + 2
    KH = HID // 2
    SSQ = 400
    MT = FF // P
    HT = SIDE * TT
    SCALE = float(DH) ** -0.5

    ctx = ExitStack()
    with ctx:
        def sb(name, shape, dt=F32):
            return ctx.enter_context(nc.sbuf_tensor(name, shape, dt))

        def sem(name):
            return ctx.enter_context(nc.semaphore(name))

        xn = sb("xn", [P, 2, PATCH * IMG])
        xT = sb("xT", [P, 2, KC * TT])
        xh = sb("xh", [P, 2, KC * TT], F32R)
        xl = sb("xl", [P, 2, KC * TT], F32R)
        wraw = sb("wraw", [P, NK, HID])
        whl = sb("whl", [P, NK, YW], F32R)
        scratch = sb("scratch", [P, NTOK * P])
        squares = scratch[:, 0:PATCH * PATCH]
        oT = scratch[0:GW, :].rearrange("p (g n b) -> p g n b", g=HQ, n=NTOK)
        ssq = sb("ssq", [P, TILES * SIDE])
        rows = sb("rows", [NK, 2, P])
        rows2 = sb("rows2", [NK, 2, P])
        gb = sb("gb", [P, 2, NK])
        ident = sb("ident", [P, P])
        sel = sb("sel", [P, BH])
        ones = sb("ones", [P, TT], F32R)
        colsum = sb("colsum", [TT, HID])
        bias1 = sb("bias1", [TT, HID])
        bc = sb("bc", [TT, 5, HID])
        st = sb("st", [TT, 32])
        t1 = sb("t1", [TT, HID])
        t2 = sb("t2", [TT, HID])
        h0 = sb("h0", [TT, TILES, HID])
        hn = sb("hn", [TT, 2, HID])
        hT = sb("hT", [KH, 2, TT])
        wqkv = sb("wqkv", [KH, 2, G5 * HID])
        wo = sb("wo", [GW, HQ, HID])
        qkv = sb("qkv", [TT, HQ * G5 * GW])
        at = [sb(f"at{i}", [P, NTOK, G5 * GW]) for i in range(HALVES)]
        vc = sb("vc", [P, NTOK, GW])
        sc = sb("sc", [P, 2, NTOK * NTOK * HPG])
        pr = sb("pr", [P, 2, NTOK * NTOK * HPG])
        mx = sb("mx", [P, 2 * NTOK, HPG])
        lam = sb("lam", [P, 2, HPG])
        oc = sb("oc", [P, NTOK, GW])
        hT2 = sb("hT2", [KH, 2, HT])
        w0T = sb("w0T", [KH, 2, FF])
        w1T = sb("w1T", [P, MT, HID])
        brow = sb("brow", [MT, P])
        b0 = sb("b0", [P, MT])
        al = sb("al", [P, 6])
        msk = sb("msk", [P, 3, 3, MT])
        cf = sb("cf", [P, 3, MT])
        cb = sb("cb", [P, 3])
        prod = wraw[:, :, :].rearrange("p a b -> p (a b)")[:, 0:NTOK * NTOK * GW]
        wfc = xn[:, 0, 0:MT * HID].rearrange("p (t e) -> p t e", t=MT)
        wpj = xn[0:KH, 0, MT * HID:MT * HID + 2 * FF].rearrange("p (k h) -> p k h", k=2)
        gT = xn[:, 1, 0:MT * HT].rearrange("p (m t) -> p m t", m=MT)

        ps = ctx.enter_context(nc.psum_tensor("ps", [P, 8, 512], F32))
        Y = [ps[:, 0, :], ps[:, 1, :]]
        QK = [ps[:, 2, :], ps[:, 3, :]]
        TR = ps[:, 4, :]
        WOB = [ps[:, 5, :], ps[:, 7, :]]
        PB, PSM = ps[:, 7, :], ps[:, 6, :]
        PREP = [ps[:, 0, :], ps[:, 1, :], ps[:, 6, :], ps[:, 7, :]]
        OTB = [ps[:, 0, :], ps[:, 1, :], ps[:, 6, :]]

        rows_in, w_in = sem("rows_in"), [sem(f"w_in{c}") for c in range(NWC)]
        x_in = [sem(f"x_in{i}") for i in range(2)]
        bc_in, wqkv_in, wo_in, ffn_in = sem("bc_in"), sem("wqkv_in"), sem("wo_in"), sem("ffn_in")
        small_in = sem("small_in")
        at_in = [sem(f"at_in{i}") for i in range(HALVES)]
        out_done = sem("out_done")
        zeroed, ident_ok, sel_ok, ones_ok, msk_ok = (sem("zeroed"), sem("ident_ok"), sem("sel_ok"),
                                                     sem("ones_ok"), sem("msk_ok"))
        rows_ok = sem("rows_ok")
        rowsT_ok, gb_ok, betaW_ok = sem("rowsT_ok"), sem("gb_ok"), sem("betaW_ok")
        wg_ok, wh_ok, wl_ok = sem("wg_ok"), sem("wh_ok"), sem("wl_ok")
        xT_ok, xh_ok, xl_ok, sq_ok = sem("xT_ok"), sem("xh_ok"), sem("xl_ok"), sem("sq_ok")
        chunk_done, y_ok, y_read = sem("chunk_done"), sem("y_ok"), sem("y_read")
        var_ok, std_ok = sem("var_ok"), sem("std_ok")
        hn_ok, tr_ok, hT_ok, qkv_ps_ok, qkv_ok = (sem("hn_ok"), sem("tr_ok"), sem("hT_ok"),
                                                  sem("qkv_ps_ok"), sem("qkv_ok"))
        sc_ok, exp_ok, oc_ok, oT_ps_ok, oT_ok = (sem("sc_ok"), sem("exp_ok"), sem("oc_ok"),
                                                 sem("oT_ps_ok"), sem("oT_ok"))
        wo_ps_ok, h1_ok = sem("wo_ps_ok"), sem("h1_ok")
        hn2_ok, tr2_ok, hT2_ok = sem("hn2_ok"), sem("tr2_ok"), sem("hT2_ok")
        fc_ok, gelu_ok, pj_ok, res_ok = sem("fc_ok"), sem("gelu_ok"), sem("pj_ok"), sem("res_ok")
        prep_ps, prep_sb, wsc_ok, w1_ok, b0_ok = (sem("prep_ps"), sem("prep_sb"), sem("wsc_ok"),
                                                  sem("w1_ok"), sem("b0_ok"))
        lam_ok, cf_ok, fb_ok, bo_ok, fbadd_ok = (sem("lam_ok"), sem("cf_ok"), sem("fb_ok"),
                                                 sem("bo_ok"), sem("fbadd_ok"))
        dve_step, act_step, pool_step = sem("dve_step"), sem("act_step"), sem("pool_step")

        block = ctx.enter_context(nc.Block())

        def load_x(eng, t, cs):
            half, hrow = t // SIDE, t % SIDE
            for c in cs:
                eng.dma_start(xn[c * BH:(c + 1) * BH, t % 2, :],
                              x[half * BH:(half + 1) * BH, c, hrow * PATCH:(hrow + 1) * PATCH, :]
                              .rearrange("b p v -> b (p v)")).then_inc(x_in[t % 2], 16)

        def load_w(eng, k, cs):
            wv = W_proj.rearrange("(p q c) n -> c q p n", q=PATCH, c=CH)
            for c in cs:
                eng.dma_start(wraw[c * PATCH:(c + 1) * PATCH, k * WC:(k + 1) * WC, :],
                              wv[c, :, k * WC:(k + 1) * WC, :]).then_inc(w_in[k], 16)

        @block.sync
        def _(sp):
            sp.dma_start(rows[:, 0, :], ln1_g.rearrange("(p k) -> p k", k=P)).then_inc(rows_in, 16)
            sp.dma_start(rows[:, 1, :], ln1_b.rearrange("(p k) -> p k", k=P)).then_inc(rows_in, 16)
            load_w(sp, 0, (0, 1))
            load_x(sp, 0, (0, 1))
            for k in range(1, NWC):
                load_w(sp, k, (0, 1))
            load_x(sp, 1, (0, 1, 2, 3))
            for i, v in enumerate((b_proj, ln2_g, ln2_b, bo, b_out)):
                sp.dma_start(bc[:, i, :], v.rearrange("(a n) -> a n", a=1).partition_broadcast(TT)
                             if False else v.partition_broadcast(TT)).then_inc(bc_in, 16)
            for kt in range(2):
                for w, a, n in ((Wq, 0, 2 * HID), (Wk, 2 * HID, 2 * HID), (Wv, 4 * HID, HID)):
                    sp.dma_start(wqkv[:, kt, a:a + n], w[kt * KH:(kt + 1) * KH, :]).then_inc(wqkv_in, 16)
            sp.dma_start(wo[:, :, :], Wo.rearrange("(g e) n -> e g n", g=HQ)).then_inc(wo_in, 16)
            sp.dma_start(al[:, 0:3], alpha_e.partition_broadcast(P)).then_inc(small_in, 16)
            sp.dma_start(al[:, 3:6], alpha_r.partition_broadcast(P)).then_inc(small_in, 16)
            for g in range(HQ):
                sp.dma_start(lam[g * BH:(g + 1) * BH, 0, :],
                             lambda_p[g * HPG:(g + 1) * HPG, 0, 0].partition_broadcast(BH)).then_inc(small_in, 16)
            sp.dma_start(brow[:, :], b_fc.rearrange("(t p) -> t p", p=P)).then_inc(small_in, 16)

            def send_heads(t):
                sp.wait_ge(qkv_ok, t + 1)
                for w in range(SIDE):
                    for g in range(HQ):
                        sp.dma_start(at[t // SIDE][g * BH:(g + 1) * BH, (t % SIDE) * SIDE + w, :],
                                     qkv[w * BH:(w + 1) * BH, g * G5 * GW:(g + 1) * G5 * GW])\
                            .then_inc(at_in[t // SIDE], 16)

            for t in range(TILES):
                if t + 2 < TILES:
                    sp.wait_ge(xT_ok, 2 * (t + 1))
                    sp.wait_ge(sq_ok, SIDE * (t + 1))
                    load_x(sp, t + 2, range(CH))
                if t + 2 == TILES:
                    sp.wait_ge(xT_ok, 2 * (t + 1))
                    sp.wait_ge(sq_ok, SIDE * (t + 1))
                    sp.dma_start(wfc, w_fc.rearrange("(t p) e -> p t e", p=P)).then_inc(ffn_in, 16)
                    sp.dma_start(wpj, w_out.rearrange("(k e) h -> e k h", k=2)).then_inc(ffn_in, 16)
                if t >= 1:
                    send_heads(t - 1)
            send_heads(TILES - 1)
            for t in range(TILES):
                sp.wait_ge(res_ok, t + 1)
                half, hrow = t // SIDE, t % SIDE
                for w in range(SIDE):
                    sp.dma_start(out[half * BH:(half + 1) * BH, hrow * SIDE + w, :],
                                 h0[w * BH:(w + 1) * BH, t, :]).then_inc(out_done, 16)
            sp.wait_ge(out_done, 16 * SIDE * TILES)

        @block.gpsimd
        def _(pool):
            pool.memset(ident[:, :], 0.0).then_inc(zeroed, 1)
            pool.wait_ge(zeroed, 1)
            pool.affine_select(out=ident[:, :], in_=ident[:, :], compare_op=ALU.not_equal, fill=1.0, base=0,
                               pattern=[[-1, P]], channel_multiplier=1).then_inc(ident_ok, 1)
            pool.memset(msk[:, :, :, :], 1.0).then_inc(zeroed, 1)
            pool.wait_ge(zeroed, 2)
            for i, e in enumerate(EMBED):
                for j, r in enumerate(RATIO):
                    pool.affine_select(out=msk[:, i, j, :], in_=msk[:, i, j, :], compare_op=ALU.is_gt, fill=0.0,
                                       base=r * e, pattern=[[-P, MT]], channel_multiplier=-1).then_inc(msk_ok, 1)
            for k in range(NWC):
                pool.wait_ge(wh_ok, k + 1)
                s = slice(k * WC, (k + 1) * WC)
                pool.tensor_tensor(whl[:, s, LO:YW], wraw[:, s, :], whl[:, s, 0:HID].bitcast(F32),
                                   ALU.subtract).then_inc(wl_ok, 1)
            for t in range(TILES):
                for kc in range(2):
                    pool.wait_ge(xh_ok, 2 * t + kc + 1)
                    pool.tensor_tensor(xl[:, kc, :], xT[:, kc, :], xh[:, kc, :].bitcast(F32),
                                       ALU.subtract).then_inc(xl_ok, 1)
            n = [0]

            def step(ins):
                n[0] += 1
                ins.then_inc(pool_step, 1)
                pool.wait_ge(pool_step, n[0])

            pool.wait_ge(cf_ok, 1)
            pool.wait_ge(ffn_in, 32)
            e0 = 0
            for k, e1 in enumerate(EMBED):
                v = wfc[:, :, e0:e1]
                pool.tensor_tensor(v, v, cf[:, k, :].unsqueeze(2).to_broadcast([P, MT, e1 - e0]),
                                   ALU.mult).then_inc(wsc_ok, 1)
                e0 = e1
            pool.wait_ge(prep_sb, 7)
            e0 = 0
            for k, e1 in enumerate(EMBED):
                v = w1T[:, :, e0:e1]
                pool.tensor_tensor(v, v, cf[:, k, :].unsqueeze(2).to_broadcast([P, MT, e1 - e0]),
                                   ALU.mult).then_inc(w1_ok, 1)
                e0 = e1
            for t in range(TILES):
                pool.wait_ge(hn_ok, t + 1)
                pool.tensor_tensor(h0[:, t, :], h0[:, t, :], bc[:, 3, :], ALU.add).then_inc(bo_ok, 1)
            pool.wait_ge(fb_ok, 3)
            for t in range(TILES):
                pool.wait_ge(hn2_ok, t + 1)
                pool.tensor_tensor(h0[:, t, :], h0[:, t, :], bc[:, 4, :], ALU.add).then_inc(fbadd_ok, 1)

        @block.scalar
        def _(act):
            lns = [0]

            def sqrt_():
                lns[0] += 1
                act.wait_ge(var_ok, lns[0])
                act.activation(st[:, 17:18], st[:, 16:17], ACT.Sqrt).then_inc(std_ok, 1)

            def split_high(t, kc):
                c = 2 * t + kc
                act.wait_ge(xT_ok, c + 1)
                if c >= 2:
                    act.wait_ge(chunk_done, c - 1)
                act.activation(xh[:, kc, :], xT[:, kc, :], ACT.Copy).then_inc(xh_ok, 1)

            def square(t):
                act.wait_ge(x_in[t % 2], 64 * (t // 2 + 1))
                v = xn[:, t % 2, :].rearrange("p (r w q) -> p w r q", w=SIDE, q=PATCH)
                for w in range(SIDE):
                    if SIDE * t + w:
                        act.wait_ge(sq_ok, SIDE * t + w)
                    act.activation(squares.rearrange("p (r q) -> p r q", q=PATCH), v[:, w], ACT.Square,
                                   accum_out=ssq[:, SIDE * t + w:SIDE * t + w + 1]).then_inc(sq_ok, 1)

            def hT_copy(t):
                act.wait_ge(tr_ok, t + 1)
                act.activation(hT[:, :, :].rearrange("p k t -> p (k t)"), TR[0:KH, 0:2 * TT],
                               ACT.Copy).then_inc(hT_ok, 1)

            def qkv_copy(t):
                act.wait_ge(qkv_ps_ok, t + 1)
                if t:
                    act.wait_ge(at_in[(t - 1) // SIDE], 16 * SIDE * HQ * ((t - 1) % SIDE + 1))
                w = 2 * G5 * GW
                act.activation(qkv[:, 0:w], QK[0][0:TT, 0:w], ACT.Copy).then_inc(act_step, 1)
                act.activation(qkv[:, w:2 * w], QK[1][0:TT, 0:w], ACT.Copy).then_inc(qkv_ok, 1)

            load_w(act, 0, (2, 3))
            load_x(act, 0, (2, 3))
            for k in range(1, NWC):
                load_w(act, k, (2, 3))
            act.wait_ge(wg_ok, 1)
            for k in range(NWC):
                act.wait_ge(wg_ok, k + 1)
                s = slice(k * WC, (k + 1) * WC)
                act.activation(whl[:, s, 0:HID], wraw[:, s, :], ACT.Copy).then_inc(wh_ok, 1)
                if k == 0:
                    split_high(0, 0)
                    split_high(0, 1)
            square(0)
            split_high(1, 0)
            split_high(1, 1)
            square(1)
            for t in range(TILES):
                for _ in range(3):
                    sqrt_()
                if t >= 1:
                    qkv_copy(t - 1)
                if t + 2 < TILES:
                    split_high(t + 2, 0)
                hT_copy(t)
                if t + 2 < TILES:
                    split_high(t + 2, 1)
                    square(t + 2)
                if t == TILES - 1:
                    qkv_copy(t)
            for i in range(8):
                act.wait_ge(prep_ps, i + 1)
                src = PREP[i % 4]
                if i < 4:
                    a, n = (0, 4 * P) if i % 2 == 0 else (4 * P, 2 * P)
                    act.activation(w0T[:, i // 2, a:a + n], src[0:KH, 0:n], ACT.Copy).then_inc(prep_sb, 1)
                elif i < 7:
                    a = 2 * (i - 4)
                    act.activation(w1T[:, a:a + 2, :].rearrange("p t e -> p (t e)"), src[:, 0:2 * HID],
                                   ACT.Copy).then_inc(prep_sb, 1)
                else:
                    act.activation(b0[:, :], src[:, 0:MT], ACT.Copy).then_inc(prep_sb, 1)
            act.wait_ge(small_in, 16 * 7)
            act.activation(lam[:, 1, :], lam[:, 0, :], ACT.Exp).then_inc(lam_ok, 1)

            def exp_(half):
                act.wait_ge(sc_ok, half + 1)
                act.activation(pr[:, :, :].rearrange("p a b -> p (a b)"), sc[:, :, :].rearrange("p a b -> p (a b)"),
                               ACT.Exp, scale=SCALE).then_inc(exp_ok, 1)

            def post(half):
                for i in range(3):
                    act.wait_ge(oT_ps_ok, 3 * half + i + 1)
                    n = min(4, NTOK - 4 * i)
                    act.activation(oT[:, :, 4 * i:4 * i + n, :].rearrange("p g n b -> p n g b"),
                                   OTB[i][0:GW, 0:n * P].rearrange("p (n g b) -> p n g b", g=HQ, b=BH),
                                   ACT.Copy).then_inc(oT_ok, 1)
                for i in range(SIDE):
                    sqrt_()
                    act.wait_ge(tr2_ok, SIDE * half + i + 1)
                    act.activation(hT2[:, :, i * TT:(i + 1) * TT],
                                   TR[0:KH, 0:2 * TT].rearrange("p (k t) -> p k t", k=2),
                                   ACT.Copy).then_inc(hT2_ok, 1)
                act.wait_ge(b0_ok, 1)
                for m in range(MT):
                    act.wait_ge(fc_ok, MT * half + m + 1)
                    if half:
                        act.wait_ge(pj_ok, SIDE)
                    act.activation(gT[:, m, :], QK[m % 2][:, 0:HT], ACT.Gelu_apprx_tanh,
                                   bias=b0[:, m:m + 1]).then_inc(gelu_ok, 1)

            exp_(0)
            post(0)
            exp_(1)
            post(1)

        @block.vector
        def _(dve):
            n = [0]

            def step(ins):
                n[0] += 1
                ins.then_inc(dve_step, 1)
                dve.wait_ge(dve_step, n[0])

            lns = [0]

            def rstd():
                lns[0] += 1
                dve.wait_ge(std_ok, lns[0])
                step(dve.reciprocal(st[:, 18:19], st[:, 17:18]))

            def turn(t):
                dve.wait_ge(x_in[t % 2], 64 * (t // 2 + 1))
                for kc in range(2):
                    c = 2 * t + kc
                    if c >= 2:
                        dve.wait_ge(xl_ok, c - 1)
                    w = KC * TT
                    dve.transpose(xT[:, kc, :], xn[:, t % 2, kc * w:(kc + 1) * w]).then_inc(xT_ok, 1)

            def row_norm(src):
                step(dve.bn_stats(st[:, 0:6], src))
                step(dve.bn_aggr(st[:, 6:8], st[:, 0:6]))
                dve.tensor_scalar(st[:, 16:17], st[:, 7:8], EPS, None, ALU.add).then_inc(var_ok, 1)
                rstd()

            def embed_norm(t):
                y = Y[t % 2]
                dve.wait_ge(y_ok, t + 1)
                if t == 0:
                    step(dve.tensor_copy(t1[:, :], PSM[0:TT, LO:YW]))
                    dve.wait_ge(bc_in, 16 * 5)
                    dve.tensor_tensor(colsum[:, :], t1[:, :], PSM[0:TT, 0:HID], ALU.add)
                    step(dve.tensor_tensor(bias1[:, :], bc[:, 0, :], PB[0:TT, 0:HID], ALU.add))
                step(dve.tensor_scalar(st[:, 8:9], y[0:TT, HID:HID + 1], -1.0 / D1, None, ALU.mult))
                step(dve.tensor_scalar(st[:, 9:10], st[:, 8:9], st[:, 8:9], EPS, ALU.mult, ALU.subtract))
                dve.scalar_tensor_tensor(out=st[:, 16:17], in0=y[0:TT, SSQ:SSQ + 1], scalar=1.0 / D1,
                                         in1=st[:, 9:10], op0=ALU.mult, op1=ALU.subtract).then_inc(var_ok, 1)
                step(dve.scalar_tensor_tensor(out=t1[:, :], in0=colsum[:, :], scalar=st[:, 8:9],
                                              in1=y[0:TT, 0:HID], op0=ALU.mult, op1=ALU.add))
                dve.tensor_tensor(t2[:, :], t1[:, :], y[0:TT, LO:YW], ALU.add).then_inc(y_read, 1)
                rstd()
                dve.wait_ge(y_read, t + 1)
                step(dve.scalar_tensor_tensor(out=t1[:, :], in0=t2[:, :], scalar=st[:, 18:19], in1=bias1[:, :],
                                              op0=ALU.mult, op1=ALU.add))
                row_norm(t1[:, :])
                step(dve.tensor_scalar(t2[:, :], t1[:, :], st[:, 6:7], st[:, 18:19], ALU.subtract, ALU.mult))
                step(dve.tensor_tensor(t1[:, :], t2[:, :], bc[:, 1, :], ALU.mult))
                step(dve.tensor_tensor(h0[:, t, :], t1[:, :], bc[:, 2, :], ALU.add))
                row_norm(h0[:, t, :])
                if t >= 2:
                    dve.wait_ge(tr_ok, t - 1)
                dve.tensor_scalar(hn[:, t % 2, :], h0[:, t, :], st[:, 6:7], st[:, 18:19], ALU.subtract,
                                  ALU.mult).then_inc(hn_ok, 1)
                dve.wait_ge(hn_ok, t + 1)

            def scores(half, m):
                a = at[half]
                if m == 0:
                    dve.wait_ge(at_in[half], 16 * SIDE * HQ * SIDE)
                v = prod.rearrange("p (n m e) -> p n m e", n=NTOK, m=NTOK)
                q = a[:, :, m * GW:(m + 1) * GW].unsqueeze(2).to_broadcast([P, NTOK, NTOK, GW])
                k = a[:, :, (2 + m) * GW:(3 + m) * GW].unsqueeze(1).to_broadcast([P, NTOK, NTOK, GW])
                step(dve.tensor_tensor(v, q, k, ALU.mult))

            def sum_d(m):
                step(dve.tensor_reduce(sc[:, m, :], prod.rearrange("p (a d) -> p a d", d=DH), AX_X, ALU.add))

            def by_row(v):
                return v.rearrange("p a (n m h) -> p (a n) m h", n=NTOK, m=NTOK)

            def softmax_max(half):
                s = by_row(sc[:, :, :])
                step(dve.tensor_reduce(mx[:, :, :], s.rearrange("p a m h -> p a h m"), AX_X, ALU.max))
                dve.tensor_tensor(s, s, mx[:, :, :].unsqueeze(2).to_broadcast([P, 2 * NTOK, NTOK, HPG]),
                                  ALU.subtract).then_inc(sc_ok, 1)

            def softmax_mix(half):
                e = by_row(pr[:, :, :])
                dve.wait_ge(exp_ok, half + 1)
                step(dve.tensor_reduce(mx[:, :, :], e.rearrange("p a m h -> p a h m"), AX_X, ALU.add))
                step(dve.reciprocal(mx[:, :, :], mx[:, :, :]))
                dve.wait_ge(lam_ok, 1)
                r1 = mx[:, NTOK:2 * NTOK, :]
                step(dve.tensor_tensor(r1, r1, lam[:, 1, :].unsqueeze(1).to_broadcast([P, NTOK, HPG]), ALU.mult))
                step(dve.tensor_tensor(e, e, mx[:, :, :].unsqueeze(2).to_broadcast([P, 2 * NTOK, NTOK, HPG]),
                                       ALU.mult))
                step(dve.tensor_copy(vc[:, :, :], at[half][:, :, 4 * GW:5 * GW]))
                step(dve.tensor_tensor(pr[:, 0, :], pr[:, 0, :], pr[:, 1, :], ALU.subtract))

            def values(half):
                pw = pr[:, 0, :].rearrange("p (n a) -> p n a", n=NTOK).unsqueeze(3)\
                    .to_broadcast([P, NTOK, NTOK * HPG, DH])
                vv = vc[:, :, :].rearrange("p m (h d) -> p (m h) d", d=DH).unsqueeze(1)\
                    .to_broadcast([P, NTOK, NTOK * HPG, DH])
                step(dve.tensor_tensor(prod.rearrange("p (n a d) -> p n a d", n=NTOK, d=DH), pw, vv, ALU.mult))

            def sum_m(half):
                if half:
                    dve.wait_ge(oT_ps_ok, 3)
                dve.tensor_reduce(oc[:, :, :], prod.rearrange("p (n m e) -> p n e m", n=NTOK, m=NTOK), AX_X,
                                  ALU.add).then_inc(oc_ok, 1)
                dve.wait_ge(oc_ok, half + 1)

            def attn_residual_norm(t):
                dve.wait_ge(wo_ps_ok, t + 1)
                dve.wait_ge(bo_ok, t + 1)
                dve.tensor_tensor(h0[:, t, :], h0[:, t, :], WOB[t % 2][0:TT, 0:HID], ALU.add).then_inc(h1_ok, 1)
                dve.wait_ge(h1_ok, t + 1)
                row_norm(h0[:, t, :])
                if t >= 2:
                    dve.wait_ge(tr2_ok, t - 1)
                dve.tensor_scalar(hn[:, t % 2, :], h0[:, t, :], st[:, 6:7], st[:, 18:19], ALU.subtract,
                                  ALU.mult).then_inc(hn2_ok, 1)
                dve.wait_ge(hn2_ok, t + 1)

            def ffn_residual(t):
                dve.wait_ge(pj_ok, t + 1)
                dve.wait_ge(fbadd_ok, t + 1)
                dve.tensor_tensor(h0[:, t, :], h0[:, t, :], WOB[t % 2][0:TT, 0:HID], ALU.add).then_inc(res_ok, 1)

            dve.wait_ge(ident_ok, 1)
            dve.tensor_reduce(sel[:, :], ident[:, :].rearrange("p (c b) -> p b c", b=BH), AX_X,
                              ALU.add).then_inc(sel_ok, 1)
            dve.memset(ones[:, :].bitcast(F32), 1.0).then_inc(ones_ok, 1)
            dve.memset(whl[:, :, HID:LO].bitcast(F32), 1.0).then_inc(ones_ok, 1)
            dve.wait_ge(rows_in, 32)
            dve.tensor_copy(rows2[:, :, :].rearrange("p i (c q) -> p i q c", c=CH),
                            rows[:, :, :].rearrange("p i (q c) -> p i q c", c=CH)).then_inc(rows_ok, 1)
            dve.wait_ge(rowsT_ok, 1)
            dve.tensor_copy(gb[:, :, :].rearrange("p a b -> p (a b)"), TR[:, 0:2 * NK]).then_inc(gb_ok, 1)
            dve.wait_ge(gb_ok, 1)
            for k in range(NWC):
                dve.wait_ge(betaW_ok, k + 1)
                s = slice(k * WC, (k + 1) * WC)
                dve.tensor_tensor(wraw[:, s, :], wraw[:, s, :],
                                  gb[:, 0, s].unsqueeze(2).to_broadcast([P, WC, HID]), ALU.mult).then_inc(wg_ok, 1)
                if k == 0:
                    turn(0)
            turn(1)
            embed_norm(0)
            dve.wait_ge(small_in, 16 * 7)
            dve.wait_ge(msk_ok, 9)
            for j in range(3):
                step(dve.tensor_scalar(msk[:, :, j, :], msk[:, :, j, :], al[:, 3 + j:4 + j], None, ALU.mult))
            step(dve.tensor_tensor(cf[:, :, :], msk[:, :, 0, :], msk[:, :, 1, :], ALU.add))
            step(dve.tensor_tensor(cf[:, :, :], cf[:, :, :], msk[:, :, 2, :], ALU.add))
            for i in range(3):
                step(dve.tensor_scalar(cf[:, i, :], cf[:, i, :], al[:, i:i + 1], None, ALU.mult))
            step(dve.tensor_tensor(cf[:, 1, :], cf[:, 1, :], cf[:, 2, :], ALU.add))
            dve.tensor_tensor(cf[:, 0, :], cf[:, 0, :], cf[:, 1, :], ALU.add).then_inc(cf_ok, 1)
            step(dve.tensor_reduce(cb[:, 0:1], al[:, 3:6], AX_X, ALU.add))
            step(dve.tensor_scalar(al[:, 0:3], al[:, 0:3], cb[:, 0:1], None, ALU.mult))
            step(dve.tensor_tensor(al[:, 1:2], al[:, 1:2], al[:, 2:3], ALU.add))
            step(dve.tensor_tensor(al[:, 0:1], al[:, 0:1], al[:, 1:2], ALU.add))
            e0 = 0
            for k, e1 in enumerate(EMBED):
                dve.tensor_scalar(bc[:, 4, e0:e1], bc[:, 4, e0:e1], al[0:TT, k:k + 1], None,
                                  ALU.mult).then_inc(fb_ok, 1)
                e0 = e1
            turn(2)
            embed_norm(1)
            turn(3)
            embed_norm(2)
            turn(4)
            embed_norm(3)
            turn(5)
            scores(0, 0)
            sum_d(0)
            embed_norm(4)
            scores(0, 1)
            embed_norm(5)
            sum_d(1)
            softmax_max(0)
            dve.wait_ge(prep_sb, 8)
            dve.tensor_tensor(b0[:, :], b0[:, :], cf[:, 0, :], ALU.mult).then_inc(b0_ok, 1)
            softmax_mix(0)
            values(0)
            sum_m(0)
            scores(1, 0)
            sum_d(0)
            for t in range(SIDE):
                attn_residual_norm(t)
            scores(1, 1)
            sum_d(1)
            softmax_max(1)
            for t in range(SIDE):
                ffn_residual(t)
            softmax_mix(1)
            values(1)
            sum_m(1)
            for t in range(SIDE, TILES):
                attn_residual_norm(t)
            for t in range(SIDE, TILES):
                ffn_residual(t)

        @block.tensor
        def _(pe):
            pe.wait_ge(ident_ok, 1)
            pe.wait_ge(rows_ok, 1)
            for i in range(2):
                last = pe.transpose(TR[:, i * NK:(i + 1) * NK], rows2[:, i, :], ident[0:NK, 0:NK])
            last.then_inc(rowsT_ok, 1)
            pe.wait_ge(gb_ok, 1)
            for k in range(NK):
                if k % WC == 0:
                    pe.wait_ge(w_in[k // WC], 64)
                last = pe.matmul(PB[0:TT, 0:HID], gb[:, 1, k:k + 1].to_broadcast([P, TT]), wraw[:, k, :],
                                 start=(k == 0), stop=(k == NK - 1))
                if k % WC == WC - 1:
                    last.then_inc(betaW_ok, 1)

            def project(t, upto):
                y = Y[t % 2]
                for k in range(*upto):
                    c = 2 * t + k // KC
                    if k % KC == 0:
                        pe.wait_ge(xl_ok, c + 1)
                    if k == 0 and t >= 2:
                        pe.wait_ge(y_read, t - 1)
                    if t == 0 and k % WC == 0:
                        pe.wait_ge(wl_ok, k // WC + 1)
                    if t == 0 and k == 0:
                        pe.wait_ge(ones_ok, 2)
                    if t == 0:
                        pe.matmul(PSM[0:TT, 0:YW], ones[:, :], whl[:, k, :], start=(k == 0), stop=(k == NK - 1))
                    s = slice((k % KC) * TT, (k % KC + 1) * TT)
                    pe.matmul(y[0:TT, 0:YW], xh[:, k // KC, s], whl[:, k, :], start=(k == 0), stop=False)
                    last = pe.matmul(y[0:TT, 0:LO], xl[:, k // KC, s], whl[:, k, 0:LO], start=False,
                                     stop=(k == NK - 1))
                    if k % KC == KC - 1:
                        last.then_inc(chunk_done, 1)

            def sum_squares(t):
                pe.wait_ge(sq_ok, SIDE * (t + 1))
                pe.wait_ge(sel_ok, 1)
                for w in range(SIDE):
                    last = pe.matmul(Y[t % 2][w * BH:(w + 1) * BH, SSQ:SSQ + 1], sel[:, :],
                                     ssq[:, SIDE * t + w:SIDE * t + w + 1], start=True, stop=True)
                last.then_inc(y_ok, 1)

            def turn_rows(t):
                pe.wait_ge(hn_ok, t + 1)
                if t:
                    pe.wait_ge(hT_ok, t)
                for k in range(2):
                    last = pe.transpose(TR[0:KH, k * TT:(k + 1) * TT], hn[:, t % 2, k * KH:(k + 1) * KH],
                                        ident[0:TT, 0:TT])
                last.then_inc(tr_ok, 1)

            def heads(t):
                pe.wait_ge(hT_ok, t + 1)
                if t == 0:
                    pe.wait_ge(wqkv_in, 16 * 6)
                else:
                    pe.wait_ge(qkv_ok, t)
                w = wqkv[:, :, :].rearrange("p k (g h e) -> p k h g e", g=G5, h=HQ)
                for b in range(2):
                    for k in range(2):
                        last = pe.matmul(QK[b][0:TT, 0:2 * G5 * GW].rearrange("p (h g e) -> p h g e", h=2, g=G5)
                                         if False else QK[b][0:TT, 0:2 * G5 * GW],
                                         hT[:, k, :], w[:, k, 2 * b:2 * b + 2], start=(k == 0), stop=(k == 1))
                last.then_inc(qkv_ps_ok, 1)

            project(0, (0, NK))
            sum_squares(0)
            for t in range(1, TILES):
                project(t, (0, 3 * NK // 4))
                turn_rows(t - 1)
                project(t, (3 * NK // 4, NK))
                sum_squares(t)
                heads(t - 1)
            turn_rows(TILES - 1)
            heads(TILES - 1)
            pe.wait_ge(y_read, TILES)
            for i in range(8):
                if i >= 4:
                    pe.wait_ge(prep_sb, i - 3)
                dst = PREP[i % 4]
                if i < 4:
                    if i == 0:
                        pe.wait_ge(wsc_ok, 3)
                    ts = range(4) if i % 2 == 0 else range(4, 6)
                    for j, m in enumerate(ts):
                        last = pe.transpose(dst[0:KH, j * P:(j + 1) * P],
                                            wfc[:, m, (i // 2) * KH:(i // 2 + 1) * KH], ident[:, :])
                elif i < 7:
                    for j in range(2):
                        m = 2 * (i - 4) + j
                        for k in range(2):
                            a = j * HID + k * KH
                            last = pe.transpose(dst[:, a:a + KH], wpj[:, k, m * P:(m + 1) * P], ident[0:KH, 0:KH])
                else:
                    pe.wait_ge(small_in, 16 * 7)
                    last = pe.transpose(dst[:, 0:MT], brow[:, :], ident[0:MT, 0:MT])
                last.then_inc(prep_ps, 1)

            def post(half):
                pe.wait_ge(oc_ok, half + 1)
                pe.wait_ge(prep_sb, 8)
                for i in range(3):
                    for j in range(min(4, NTOK - 4 * i)):
                        last = pe.transpose(OTB[i][0:GW, j * P:(j + 1) * P], oc[:, 4 * i + j, :], ident[:, :])
                    last.then_inc(oT_ps_ok, 1)
                pe.wait_ge(wo_in, 16)
                for i in range(SIDE):
                    t = SIDE * half + i
                    pe.wait_ge(oT_ok, 3 * half + (3 * i + 2) // 4 + 1)
                    if i >= 2:
                        pe.wait_ge(h1_ok, t - 1)
                    if half and i < 2:
                        pe.wait_ge(res_ok, SIDE)
                    for g in range(HQ):
                        last = pe.matmul(WOB[t % 2][0:TT, 0:HID],
                                         oT[:, g, SIDE * i:SIDE * (i + 1), :].rearrange("p n b -> p (n b)"),
                                         wo[:, g, :],
                                         start=(g == 0), stop=(g == HQ - 1))
                    last.then_inc(wo_ps_ok, 1)
                for i in range(SIDE):
                    t = SIDE * half + i
                    pe.wait_ge(hn2_ok, t + 1)
                    if t:
                        pe.wait_ge(hT2_ok, t)
                    else:
                        pe.wait_ge(hT_ok, TILES)
                    for k in range(2):
                        last = pe.transpose(TR[0:KH, k * TT:(k + 1) * TT], hn[:, t % 2, k * KH:(k + 1) * KH],
                                            ident[0:TT, 0:TT])
                    last.then_inc(tr2_ok, 1)
                pe.wait_ge(hT2_ok, SIDE * (half + 1))
                for m in range(MT):
                    if m >= 2:
                        pe.wait_ge(gelu_ok, MT * half + m - 1)
                    elif half:
                        pe.wait_ge(gelu_ok, MT)
                    else:
                        pe.wait_ge(qkv_ok, TILES)
                    for k in range(2):
                        last = pe.matmul(QK[m % 2][:, 0:HT], w0T[:, k, m * P:(m + 1) * P], hT2[:, k, :],
                                         start=(k == 0), stop=(k == 1))
                    last.then_inc(fc_ok, 1)
                pe.wait_ge(gelu_ok, MT * (half + 1))
                pe.wait_ge(w1_ok, 3)
                for i in range(SIDE):
                    t = SIDE * half + i
                    pe.wait_ge(h1_ok, min(SIDE * (half + 1), t + 3))
                    if i >= 2:
                        pe.wait_ge(res_ok, t - 1)
                    for m in range(MT):
                        last = pe.matmul(WOB[t % 2][0:TT, 0:HID], gT[:, m, i * TT:(i + 1) * TT], w1T[:, m, :],
                                         start=(m == 0), stop=(m == MT - 1))
                    last.then_inc(pj_ok, 1)

            post(0)
            post(1)


_INS = ['x', 'L0_tok_ln1_g', 'L0_tok_ln1_b', 'L0_tok_W_proj', 'L0_tok_b_proj', 'L0_tok_ln2_g', 'L0_tok_ln2_b',
        'L0_attn_Wq', 'L0_attn_Wk', 'L0_attn_Wv', 'L0_attn_lambda_p', 'L0_attn_Wo', 'L0_attn_bo', 'L0_ffn_w_fc',
        'L0_ffn_b_fc', 'L0_ffn_w_proj', 'L0_ffn_b_proj', 'L0_ffn_alpha_e', 'L0_ffn_alpha_r']
_OUTS = [((64, 9, 192), 'float32')]


def kernel(**inputs):
    import numpy as _np
    import concourse.bacc as _bacc
    from concourse import mybir as _mybir
    from concourse.bass_utils import run_bass_kernel_spmd as _run

    nc = _bacc.Bacc("TRN2", target_bir_lowering=False, num_devices=1)
    arrays, args = {}, []
    for name in _INS:
        a = _np.ascontiguousarray(inputs[name])
        arrays[f"in_{name}_dram"] = a
        args.append(nc.dram_tensor(f"in_{name}_dram", a.shape, _mybir.dt.from_np(a.dtype), kind="ExternalInput").ap())
    for i, (shape, dtype) in enumerate(_OUTS):
        dt = _mybir.dt.from_np(_np.dtype(dtype))
        args.append(nc.dram_tensor(f"out_{i}_dram", shape, dt, kind="ExternalOutput").ap())
    vit_block(nc, *args)
    r = _run(nc, [arrays], core_ids=[0])
    got = tuple(r.results[0][f"out_{i}_dram"] for i in range(len(_OUTS)))
    return got[0]
```

```python
from contextlib import ExitStack

import concourse.bass as bass
from concourse import mybir

F32 = mybir.dt.float32
F32R = mybir.dt.float32r
ALU = mybir.AluOpType
ACT = mybir.ActivationFunctionType
AX_X = mybir.AxisListType.X

P = 128
PATCH = 32
CH = 4
D1 = CH * PATCH * PATCH
HID = 192
EPS = 1e-5
EMBED = (96, 144, 192)
RATIO = (2, 3, 4)
FF = 768


def vit_block(nc, x, ln1_g, ln1_b, W_proj, b_proj, ln2_g, ln2_b, Wq, Wk, Wv, lambda_p, Wo, bo,
              w_fc, b_fc, w_out, b_out, alpha_e, alpha_r, out):
    B, _, IMG, _ = x.shape
    SIDE = IMG // PATCH
    NTOK = SIDE * SIDE
    BH = 32
    HALVES = B // BH
    TILES = HALVES * SIDE
    TT = SIDE * BH
    HEADS = lambda_p.shape[0]
    DH = HID // HEADS
    HQ = P // BH
    HPG = HEADS // HQ
    GW = HPG * DH
    G5 = 5
    KC = 8
    SLOTS = 4
    NK = D1 // P
    WC = 8
    NC = NK // KC
    NWC = NK // WC
    YW = 2 * HID + 2
    LO = HID + 2
    KH = HID // 2
    SSQ = 400
    MT = FF // P
    HT = SIDE * TT
    SCALE = float(DH) ** -0.5
    XW = TT + 2
    PIECE = SIDE * NTOK * GW

    PIECES = [[(0, 3, 0, 3)], [(3, 3, 0, 6), (0, 3, 3, 3)], [(6, 3, 0, 9), (0, 6, 6, 3)]]

    ITEMS = sum(len(p) for p in PIECES) + 1

    ctx = ExitStack()
    with ctx:
        def sb(name, shape, dt=F32):
            return ctx.enter_context(nc.sbuf_tensor(name, shape, dt))

        def sem(name):
            return ctx.enter_context(nc.semaphore(name))

        xn = sb("xn", [P, 2, PATCH * IMG])
        xT = sb("xT", [P, SLOTS, KC * TT])
        xh = sb("xh", [P, SLOTS, KC, XW], F32R)
        xl = sb("xl", [P, SLOTS, KC, XW], F32R)
        wraw = sb("wraw", [P, NK, HID])
        whl = sb("whl", [P, NK, YW], F32R)
        squares = sb("squares", [P, PATCH * PATCH])
        oT = squares[:, 0:2 * NTOK * BH].rearrange("p (k n b) -> p k n b", k=2, n=NTOK)
        ssq = sb("ssq", [P, TILES * SIDE])
        rows = sb("rows", [NK, 2, P])
        rows2 = sb("rows2", [NK, 2, P])
        gb = sb("gb", [P, 2, NK])
        ident = sb("ident", [P, P])
        sel = sb("sel", [P, BH])
        ones = sb("ones", [P, TT])
        colsum = sb("colsum", [TT, HID])
        bias1 = sb("bias1", [TT, HID])
        bc = sb("bc", [TT, 5, HID])
        st = sb("st", [TT, 32])
        t1 = sb("t1", [TT, HID])
        t2 = sb("t2", [TT, HID])
        h0 = sb("h0", [TT, TILES, HID])
        hn = sb("hn", [TT, 2, HID])
        hT = sb("hT", [KH, 2, TT])
        wqkv = sb("wqkv", [KH, 2, G5 * HID])
        wo = sb("wo", [P, 2, HID])
        qkv = sb("qkv", [TT, HQ * G5 * GW])
        at = [sb(f"at{i}", [P, NTOK, G5 * GW]) for i in range(HALVES)]
        vc = sb("vc", [P, NTOK, GW])
        sc = sb("sc", [P, 2, NTOK * NTOK * HPG])
        pr = sb("pr", [P, 2, NTOK * NTOK * HPG])
        mx = sb("mx", [P, 2 * NTOK, HPG])
        lam = sb("lam", [P, 2, HPG])
        oc = sb("oc", [P, NTOK, GW])
        hT2 = sb("hT2", [KH, 2, HT])
        w0T = sb("w0T", [KH, 2, FF])
        w1T = sb("w1T", [P, MT, HID])
        brow = sb("brow", [MT, P])
        b0 = sb("b0", [P, MT])
        al = sb("al", [P, 6])
        msk = sb("msk", [P, 3, 3, MT])
        cf = sb("cf", [P, 3, MT])
        cb = sb("cb", [P, 3])
        flat = wraw[:, :, :].rearrange("p a b -> p (a b)")
        prod = flat[:, 0:PIECE]
        pprod = [flat[:, (1 + i) * PIECE:(2 + i) * PIECE] for i in range(2)]
        csrow = flat[TT:TT + 1, 3 * PIECE:3 * PIECE + HID]
        wfc = xn[:, 0, 0:MT * HID].rearrange("p (t e) -> p t e", t=MT)
        wpj = xn[0:KH, 0, MT * HID:MT * HID + 2 * FF].rearrange("p (k h) -> p k h", k=2)
        gT = xn[:, 1, 0:MT * HT].rearrange("p (m t) -> p m t", m=MT)

        ps = ctx.enter_context(nc.psum_tensor("ps", [P, 8, 512], F32))
        Y = [ps[:, 0, :], ps[:, 1, :]]
        QK = [ps[:, 2, :], ps[:, 3, :]]
        TR = ps[:, 4, :]
        WOB = [ps[:, 5, :], ps[:, 7, :]]
        PB, PSM = ps[:, 7, :], ps[:, 6, :]
        PREP = [ps[:, 0, :], ps[:, 1, :], ps[:, 6, :], ps[:, 7, :]]
        OTB = [ps[:, 0, :], ps[:, 1, :], ps[:, 6, :]]

        rows_in, w_in = sem("rows_in"), [sem(f"w_in{c}") for c in range(NWC)]
        x_in = [sem(f"x_in{i}") for i in range(2)]
        bc_in, wqkv_in, wo_in, ffn_in = sem("bc_in"), sem("wqkv_in"), sem("wo_in"), sem("ffn_in")
        small_in = sem("small_in")
        at_in = [sem(f"at_in{i}") for i in range(HALVES)]
        out_done = sem("out_done")
        zeroed, ident_ok, sel_ok, ones_ok, msk_ok = (sem("zeroed"), sem("ident_ok"), sem("sel_ok"),
                                                     sem("ones_ok"), sem("msk_ok"))
        rows_ok = sem("rows_ok")
        rowsT_ok, gb_ok, betaW_ok = sem("rowsT_ok"), sem("gb_ok"), sem("betaW_ok")
        wg_ok, wh_ok, wl_ok = sem("wg_ok"), sem("wh_ok"), sem("wl_ok")
        xT_ok, xh_ok, xl_ok, sq_ok = sem("xT_ok"), sem("xh_ok"), sem("xl_ok"), sem("sq_ok")
        chunk_done, y_ok, y_read = sem("chunk_done"), sem("y_ok"), sem("y_read")
        var_ok, std_ok = sem("var_ok"), sem("std_ok")
        hn_ok, tr_ok, hT_ok, qkv_ps_ok, qkv_ok = (sem("hn_ok"), sem("tr_ok"), sem("hT_ok"),
                                                  sem("qkv_ps_ok"), sem("qkv_ok"))
        sc_ok, exp_ok, oc_ok, oT_ps_ok, oT_ok = (sem("sc_ok"), sem("exp_ok"), sem("oc_ok"),
                                                 sem("oT_ps_ok"), sem("oT_ok"))
        wo_ps_ok, h1_ok = sem("wo_ps_ok"), sem("h1_ok")
        hn2_ok, tr2_ok, hT2_ok = sem("hn2_ok"), sem("tr2_ok"), sem("hT2_ok")
        fc_ok, gelu_ok, pj_ok, res_ok = sem("fc_ok"), sem("gelu_ok"), sem("pj_ok"), sem("res_ok")
        prep_ps, prep_sb, wsc_ok, w1_ok, b0_ok = (sem("prep_ps"), sem("prep_sb"), sem("wsc_ok"),
                                                  sem("w1_ok"), sem("b0_ok"))
        lam_ok, cf_ok, fb_ok, bo_ok, fbadd_ok = (sem("lam_ok"), sem("cf_ok"), sem("fb_ok"),
                                                 sem("bo_ok"), sem("fbadd_ok"))
        wlp_ok, x1s_ok, cs_ok, csb_ok, zero_ok = (sem("wlp_ok"), sem("x1s_ok"), sem("cs_ok"), sem("csb_ok"),
                                                  sem("zero_ok"))
        pprod_ok, pprod_used, mix_ok, heads_out = sem("pprod_ok"), sem("pprod_used"), sem("mix_ok"), sem("heads_out")
        dve_step, act_step, pool_step = sem("dve_step"), sem("act_step"), sem("pool_step")

        heads_dram = nc.dram_tensor("heads_dram", (HALVES, HQ, BH, NTOK, G5 * GW), F32, kind="Internal").ap()

        block = ctx.enter_context(nc.Block())

        def load_x(eng, t, cs):
            half, hrow = t // SIDE, t % SIDE
            for c in cs:
                eng.dma_start(xn[c * BH:(c + 1) * BH, t % 2, :],
                              x[half * BH:(half + 1) * BH, c, hrow * PATCH:(hrow + 1) * PATCH, :]
                              .rearrange("b p v -> b (p v)")).then_inc(x_in[t % 2], 16)

        def load_w(eng, k, cs):
            wv = W_proj.rearrange("(p q c) n -> c q p n", q=PATCH, c=CH)
            for c in cs:
                eng.dma_start(wraw[c * PATCH:(c + 1) * PATCH, k * WC:(k + 1) * WC, :],
                              wv[c, :, k * WC:(k + 1) * WC, :]).then_inc(w_in[k], 16)

        def qk(half, m, n0, nn, m0, mm):
            a, shape = at[half], [P, nn, mm, GW]
            return (a[:, n0:n0 + nn, m * GW:(m + 1) * GW].unsqueeze(2).to_broadcast(shape),
                    a[:, m0:m0 + mm, (2 + m) * GW:(3 + m) * GW].unsqueeze(1).to_broadcast(shape))

        def pv(half, i):
            shape = [P, SIDE, NTOK * HPG, DH]
            return (pr[:, 0, :].rearrange("p (n a) -> p n a", n=NTOK)[:, SIDE * i:SIDE * (i + 1)].unsqueeze(3)
                    .to_broadcast(shape),
                    vc[:, :, :].rearrange("p m (h d) -> p (m h) d", d=DH).unsqueeze(1).to_broadcast(shape))

        @block.sync
        def _(sp):
            sp.dma_start(rows[:, 0, :], ln1_g.rearrange("(p k) -> p k", k=P)).then_inc(rows_in, 16)
            sp.dma_start(rows[:, 1, :], ln1_b.rearrange("(p k) -> p k", k=P)).then_inc(rows_in, 16)
            load_w(sp, 0, (0, 1))
            load_x(sp, 0, (0, 1))
            for k in range(1, NWC):
                load_w(sp, k, (0, 1))
            load_x(sp, 1, (0, 1, 2, 3))
            for i, v in enumerate((b_proj, ln2_g, ln2_b, bo, b_out)):
                sp.dma_start(bc[:, i, :], v.partition_broadcast(TT)).then_inc(bc_in, 16)
            for kt in range(2):
                for w, a, n in ((Wq, 0, 2 * HID), (Wk, 2 * HID, 2 * HID), (Wv, 4 * HID, HID)):
                    sp.dma_start(wqkv[:, kt, a:a + n], w[kt * KH:(kt + 1) * KH, :]).then_inc(wqkv_in, 16)
            sp.wait_ge(zero_ok, 1)
            for g in range(HQ):
                a = 64 * (g % 2)
                sp.dma_start(wo[a:a + GW, g // 2, :], Wo[g * GW:(g + 1) * GW, :]).then_inc(wo_in, 16)
            sp.dma_start(al[:, 0:3], alpha_e.partition_broadcast(P)).then_inc(small_in, 16)
            sp.dma_start(al[:, 3:6], alpha_r.partition_broadcast(P)).then_inc(small_in, 16)
            for g in range(HQ):
                sp.dma_start(lam[g * BH:(g + 1) * BH, 0, :],
                             lambda_p[g * HPG:(g + 1) * HPG, 0, 0].partition_broadcast(BH)).then_inc(small_in, 16)
            sp.dma_start(brow[:, :], b_fc.rearrange("(t p) -> t p", p=P)).then_inc(small_in, 16)

            def send_heads(t):
                half, n0 = t // SIDE, (t % SIDE) * SIDE
                sp.wait_ge(qkv_ok, t + 1)
                for w in range(SIDE):
                    sp.dma_start(heads_dram[half, :, :, n0 + w, :].rearrange("g b e -> b g e"),
                                 qkv[w * BH:(w + 1) * BH, :].rearrange("b (g e) -> b g e", g=HQ))\
                        .then_inc(heads_out, 16)
                sp.wait_ge(heads_out, 16 * SIDE * (t + 1))
                sp.dma_start(at[half][:, n0:n0 + SIDE, :],
                             heads_dram[half, :, :, n0:n0 + SIDE, :].rearrange("g b n e -> (g b) n e"))\
                    .then_inc(at_in[half], 16)

            for t in range(TILES):
                if t + 2 < TILES:
                    sp.wait_ge(xT_ok, NC * (t + 1))
                    sp.wait_ge(sq_ok, SIDE * (t + 1))
                    load_x(sp, t + 2, range(CH))
                if t + 2 == TILES:
                    sp.wait_ge(xT_ok, NC * (t + 1))
                    sp.wait_ge(sq_ok, SIDE * (t + 1))
                    sp.dma_start(wfc, w_fc.rearrange("(t p) e -> p t e", p=P)).then_inc(ffn_in, 16)
                    sp.dma_start(wpj, w_out.rearrange("(k e) h -> e k h", k=2)).then_inc(ffn_in, 16)
                if t >= 1:
                    send_heads(t - 1)
            send_heads(TILES - 1)
            for t in range(TILES):
                sp.wait_ge(res_ok, t + 1)
                half, hrow = t // SIDE, t % SIDE
                for w in range(SIDE):
                    sp.dma_start(out[half * BH:(half + 1) * BH, hrow * SIDE + w, :],
                                 h0[w * BH:(w + 1) * BH, t, :]).then_inc(out_done, 16)
            sp.wait_ge(out_done, 16 * SIDE * TILES)

        @block.gpsimd
        def _(pool):
            pool.memset(ident[:, :], 0.0).then_inc(zeroed, 1)
            pool.wait_ge(zeroed, 1)
            pool.affine_select(out=ident[:, :], in_=ident[:, :], compare_op=ALU.not_equal, fill=1.0, base=0,
                               pattern=[[-1, P]], channel_multiplier=1).then_inc(ident_ok, 1)
            pool.memset(msk[:, :, :, :], 1.0).then_inc(zeroed, 1)
            pool.wait_ge(zeroed, 2)
            for i, e in enumerate(EMBED):
                for j, r in enumerate(RATIO):
                    pool.affine_select(out=msk[:, i, j, :], in_=msk[:, i, j, :], compare_op=ALU.is_gt, fill=0.0,
                                       base=r * e, pattern=[[-P, MT]], channel_multiplier=-1).then_inc(msk_ok, 1)
            def low_w(k):
                pool.wait_ge(wh_ok, k + 1)
                s = slice(k * WC, (k + 1) * WC)
                pool.tensor_tensor(whl[:, s, LO:YW], wraw[:, s, :], whl[:, s, 0:HID].bitcast(F32),
                                   ALU.subtract).then_inc(wlp_ok, 1)

            def low_x(t, *kcs):
                for kc in kcs or range(NC):
                    pool.wait_ge(xh_ok, NC * t + kc + 1)
                    pool.tensor_tensor(xl[:, kc, :, 0:TT], xT[:, kc, :].rearrange("p (k t) -> p k t", t=TT),
                                       xh[:, kc, :, 0:TT].bitcast(F32), ALU.subtract).then_inc(xl_ok, 1)

            items = [0]

            def item(out, in0, in1):
                i = items[0]
                items[0] += 1
                if i >= 2:
                    pool.wait_ge(pprod_used, i - 1)
                pool.tensor_tensor(out(pprod[i % 2]), in0, in1, ALU.mult).then_inc(pprod_ok, 1)

            def scores(t):
                half = t // SIDE
                pool.wait_ge(at_in[half], 16 * (t % SIDE + 1))
                for n0, nn, m0, mm in PIECES[t % SIDE]:
                    item(lambda b: b[:, 0:nn * mm * GW].rearrange("p (n m e) -> p n m e", n=nn, m=mm),
                         *qk(half, 1, n0, nn, m0, mm))

            def values(half):
                pool.wait_ge(mix_ok, half + 1)
                item(lambda b: b.rearrange("p (n a d) -> p n a d", n=SIDE, d=DH), *pv(half, 1))

            low_x(0, 0)
            low_w(1)
            low_x(0, 1)
            low_x(0, 2)
            low_w(3)
            low_x(0, 3)
            low_x(1)
            for t in range(2, TILES):
                low_x(t)
                if t < TILES - 1:
                    scores(t - 2)
            pool.wait_ge(cf_ok, 1)
            pool.wait_ge(ffn_in, 32)
            e0 = 0
            for k, e1 in enumerate(EMBED):
                v = wfc[:, :, e0:e1]
                pool.tensor_tensor(v, v, cf[:, k, :].unsqueeze(2).to_broadcast([P, MT, e1 - e0]),
                                   ALU.mult).then_inc(wsc_ok, 1)
                e0 = e1

            def residual_bo(t):
                pool.wait_ge(hn_ok, t + 1)
                pool.tensor_tensor(h0[:, t, :], h0[:, t, :], bc[:, 3, :], ALU.add).then_inc(bo_ok, 1)

            def residual_fb(t):
                pool.wait_ge(fb_ok, 3)
                pool.wait_ge(hn2_ok, t + 1)
                pool.tensor_tensor(h0[:, t, :], h0[:, t, :], bc[:, 4, :], ALU.add).then_inc(fbadd_ok, 1)

            for t in range(SIDE):
                residual_bo(t)
            values(0)
            scores(3)
            scores(4)
            for t in range(SIDE, TILES):
                residual_bo(t)
            scores(5)
            pool.wait_ge(prep_sb, 7)
            e0 = 0
            for k, e1 in enumerate(EMBED):
                v = w1T[:, :, e0:e1]
                pool.tensor_tensor(v, v, cf[:, k, :].unsqueeze(2).to_broadcast([P, MT, e1 - e0]),
                                   ALU.mult).then_inc(w1_ok, 1)
                e0 = e1
            for t in range(SIDE):
                residual_fb(t)
            values(1)
            for t in range(SIDE, TILES):
                residual_fb(t)

        @block.scalar
        def _(act):
            lns = [0]

            def sqrt_():
                lns[0] += 1
                act.wait_ge(var_ok, lns[0])
                act.activation(st[:, 17:18], st[:, 16:17], ACT.Sqrt).then_inc(std_ok, 1)

            def split_high(t, kc):
                c = NC * t + kc
                act.wait_ge(xT_ok, c + 1)
                if c >= SLOTS:
                    act.wait_ge(chunk_done, c - SLOTS + 1)
                act.activation(xh[:, kc, :, 0:TT], xT[:, kc, :].rearrange("p (k t) -> p k t", t=TT),
                               ACT.Copy).then_inc(xh_ok, 1)

            def square(t):
                act.wait_ge(x_in[t % 2], 64 * (t // 2 + 1))
                v = xn[:, t % 2, :].rearrange("p (r w q) -> p w r q", w=SIDE, q=PATCH)
                for w in range(SIDE):
                    if SIDE * t + w:
                        act.wait_ge(sq_ok, SIDE * t + w)
                    act.activation(squares.rearrange("p (r q) -> p r q", q=PATCH), v[:, w], ACT.Square,
                                   accum_out=ssq[:, SIDE * t + w:SIDE * t + w + 1]).then_inc(sq_ok, 1)

            def hT_copy(t):
                act.wait_ge(tr_ok, t + 1)
                act.activation(hT[:, :, :].rearrange("p k t -> p (k t)"), TR[0:KH, 0:2 * TT],
                               ACT.Copy).then_inc(hT_ok, 1)

            def qkv_copy(t):
                act.wait_ge(qkv_ps_ok, t + 1)
                if t:
                    act.wait_ge(heads_out, 16 * SIDE * t)
                w = 2 * G5 * GW
                act.activation(qkv[:, 0:w], QK[0][0:TT, 0:w], ACT.Copy).then_inc(act_step, 1)
                act.activation(qkv[:, w:2 * w], QK[1][0:TT, 0:w], ACT.Copy).then_inc(qkv_ok, 1)

            def high_w(k):
                act.wait_ge(wg_ok, k + 1)
                s = slice(k * WC, (k + 1) * WC)
                act.activation(whl[:, s, 0:HID], wraw[:, s, :], ACT.Copy).then_inc(wh_ok, 1)

            def exp_(half):
                act.wait_ge(sc_ok, half + 1)
                act.activation(pr[:, :, :].rearrange("p a b -> p (a b)"), sc[:, :, :].rearrange("p a b -> p (a b)"),
                               ACT.Exp, scale=SCALE).then_inc(exp_ok, 1)

            load_w(act, 0, (2, 3))
            load_x(act, 0, (2, 3))
            for k in range(1, NWC):
                load_w(act, k, (2, 3))
            act.wait_ge(zero_ok, 2)
            act.activation(st[0:1, 20:21], st[0:1, 21:22], ACT.Sqrt).then_inc(act_step, 1)
            high_w(0)
            split_high(0, 0)
            high_w(1)
            split_high(0, 1)
            high_w(2)
            split_high(0, 2)
            high_w(3)
            split_high(0, 3)
            square(0)
            split_high(1, 0)
            split_high(1, 1)
            split_high(1, 2)
            split_high(1, 3)
            square(1)
            for t in range(TILES):
                for _ in range(3):
                    sqrt_()
                if t >= 1:
                    qkv_copy(t - 1)
                if t + 2 < TILES:
                    split_high(t + 2, 0)
                    split_high(t + 2, 1)
                hT_copy(t)
                if t + 2 < TILES:
                    split_high(t + 2, 2)
                    square(t + 2)
                    split_high(t + 2, 3)
                if t == TILES - 1:
                    exp_(0)
                    qkv_copy(t)
            for i in range(8):
                act.wait_ge(prep_ps, i + 1)
                src = PREP[i % 4]
                if i < 4:
                    a, n = (0, 4 * P) if i % 2 == 0 else (4 * P, 2 * P)
                    act.activation(w0T[:, i // 2, a:a + n], src[0:KH, 0:n], ACT.Copy).then_inc(prep_sb, 1)
                elif i < 7:
                    a = 2 * (i - 4)
                    act.activation(w1T[:, a:a + 2, :].rearrange("p t e -> p (t e)"), src[:, 0:2 * HID],
                                   ACT.Copy).then_inc(prep_sb, 1)
                else:
                    act.activation(b0[:, :], src[:, 0:MT], ACT.Copy).then_inc(prep_sb, 1)
            act.wait_ge(small_in, 16 * 7)
            act.activation(lam[:, 1, :], lam[:, 0, :], ACT.Exp).then_inc(lam_ok, 1)

            def attention_out(half):
                for i in range(SIDE):
                    act.wait_ge(oT_ps_ok, SIDE * half + i + 1)
                    src = OTB[i][0:GW, 0:SIDE * P].rearrange("p (n k g b) -> p g k n b", k=2, g=2, b=BH)
                    for g in range(2):
                        act.activation(oT[64 * g:64 * g + GW, :, SIDE * i:SIDE * (i + 1), :], src[:, g],
                                       ACT.Copy).then_inc(oT_ok, 1)
                for i in range(SIDE):
                    sqrt_()
                    act.wait_ge(tr2_ok, SIDE * half + i + 1)
                    act.activation(hT2[:, :, i * TT:(i + 1) * TT],
                                   TR[0:KH, 0:2 * TT].rearrange("p (k t) -> p k t", k=2),
                                   ACT.Copy).then_inc(hT2_ok, 1)

            def hidden(half):
                act.wait_ge(b0_ok, 1)
                for m in range(MT):
                    act.wait_ge(fc_ok, MT * half + m + 1)
                    if half:
                        act.wait_ge(pj_ok, SIDE)
                    act.activation(gT[:, m, :], QK[m % 2][:, 0:HT], ACT.Gelu_apprx_tanh,
                                   bias=b0[:, m:m + 1]).then_inc(gelu_ok, 1)

            attention_out(0)
            exp_(1)
            hidden(0)
            attention_out(1)
            hidden(1)

        @block.vector
        def _(dve):
            n = [0]

            def step(ins):
                n[0] += 1
                ins.then_inc(dve_step, 1)
                dve.wait_ge(dve_step, n[0])

            lns = [0]

            def rstd():
                lns[0] += 1
                dve.wait_ge(std_ok, lns[0])
                step(dve.reciprocal(st[:, 18:19], st[:, 17:18]))

            def turn(t, *kcs):
                dve.wait_ge(x_in[t % 2], 64 * (t // 2 + 1))
                for kc in kcs or range(NC):
                    c = NC * t + kc
                    if c >= SLOTS:
                        dve.wait_ge(xl_ok, c - SLOTS + 1)
                    w = KC * TT
                    dve.transpose(xT[:, kc, :], xn[:, t % 2, kc * w:(kc + 1) * w]).then_inc(xT_ok, 1)

            def row_norm(src):
                step(dve.bn_stats(st[:, 0:6], src))
                step(dve.bn_aggr(st[:, 6:8], st[:, 0:6]))
                dve.tensor_scalar(st[:, 16:17], st[:, 7:8], EPS, None, ALU.add).then_inc(var_ok, 1)
                rstd()

            def embed_norm(t):
                y = Y[t % 2]
                dve.wait_ge(y_ok, t + 1)
                if t == 0:
                    step(dve.tensor_copy(csrow, y[TT:TT + 1, 0:HID]))
                    dve.tensor_tensor(csrow, csrow, y[TT:TT + 1, LO:YW], ALU.add).then_inc(cs_ok, 1)
                    dve.wait_ge(bc_in, 16 * 5)
                    dve.tensor_tensor(bias1[:, :], bc[:, 0, :], PB[0:TT, 0:HID], ALU.add)
                    dve.wait_ge(csb_ok, 1)
                    step(dve.tensor_copy(colsum[:, :], PSM[0:TT, 0:HID]))
                step(dve.tensor_scalar(st[:, 8:9], y[0:TT, HID:HID + 1], -1.0 / D1, None, ALU.mult))
                step(dve.tensor_scalar(st[:, 9:10], st[:, 8:9], st[:, 8:9], EPS, ALU.mult, ALU.subtract))
                dve.scalar_tensor_tensor(out=st[:, 16:17], in0=y[0:TT, SSQ:SSQ + 1], scalar=1.0 / D1,
                                         in1=st[:, 9:10], op0=ALU.mult, op1=ALU.subtract).then_inc(var_ok, 1)
                step(dve.scalar_tensor_tensor(out=t1[:, :], in0=colsum[:, :], scalar=st[:, 8:9],
                                              in1=y[0:TT, 0:HID], op0=ALU.mult, op1=ALU.add))
                dve.tensor_tensor(t2[:, :], t1[:, :], y[0:TT, LO:YW], ALU.add).then_inc(y_read, 1)
                rstd()
                dve.wait_ge(y_read, t + 1)
                step(dve.scalar_tensor_tensor(out=t1[:, :], in0=t2[:, :], scalar=st[:, 18:19], in1=bias1[:, :],
                                              op0=ALU.mult, op1=ALU.add))
                row_norm(t1[:, :])
                step(dve.tensor_scalar(t2[:, :], t1[:, :], st[:, 6:7], st[:, 18:19], ALU.subtract, ALU.mult))
                step(dve.tensor_tensor(t1[:, :], t2[:, :], bc[:, 1, :], ALU.mult))
                step(dve.tensor_tensor(h0[:, t, :], t1[:, :], bc[:, 2, :], ALU.add))
                row_norm(h0[:, t, :])
                if t >= 2:
                    dve.wait_ge(tr_ok, t - 1)
                dve.tensor_scalar(hn[:, t % 2, :], h0[:, t, :], st[:, 6:7], st[:, 18:19], ALU.subtract,
                                  ALU.mult).then_inc(hn_ok, 1)
                dve.wait_ge(hn_ok, t + 1)

            used = [0]

            def sum_items(out, view):
                used[0] += 1
                dve.wait_ge(pprod_ok, used[0])
                dve.tensor_reduce(out, view(pprod[(used[0] - 1) % 2]), AX_X, ALU.add).then_inc(pprod_used, 1)
                dve.wait_ge(pprod_used, used[0])

            def scores(t):
                half = t // SIDE
                dve.wait_ge(at_in[half], 16 * (t % SIDE + 1))
                if half:
                    dve.wait_ge(exp_ok, half)
                for n0, nn, m0, mm in PIECES[t % SIDE]:
                    def view(b):
                        return b[:, 0:nn * mm * GW].rearrange("p (n a d) -> p n a d", n=nn, d=DH)

                    def out(m):
                        return sc[:, m, :].rearrange("p (n a) -> p n a", n=NTOK)[:, n0:n0 + nn,
                                                                                m0 * HPG:(m0 + mm) * HPG]
                    q, k = qk(half, 0, n0, nn, m0, mm)
                    step(dve.tensor_tensor(prod[:, 0:nn * mm * GW].rearrange("p (n m e) -> p n m e", n=nn, m=mm),
                                           q, k, ALU.mult))
                    step(dve.tensor_reduce(out(0), view(prod), AX_X, ALU.add))
                    sum_items(out(1), view)

            def by_row(v):
                return v.rearrange("p a (n m h) -> p (a n) m h", n=NTOK, m=NTOK)

            def softmax_max(half):
                s = by_row(sc[:, :, :])
                step(dve.tensor_reduce(mx[:, :, :], s.rearrange("p a m h -> p a h m"), AX_X, ALU.max))
                dve.tensor_tensor(s, s, mx[:, :, :].unsqueeze(2).to_broadcast([P, 2 * NTOK, NTOK, HPG]),
                                  ALU.subtract).then_inc(sc_ok, 1)

            def softmax_mix(half):
                e = by_row(pr[:, :, :])
                dve.wait_ge(exp_ok, half + 1)
                step(dve.tensor_reduce(mx[:, :, :], e.rearrange("p a m h -> p a h m"), AX_X, ALU.add))
                step(dve.reciprocal(mx[:, :, :], mx[:, :, :]))
                dve.wait_ge(lam_ok, 1)
                r1 = mx[:, NTOK:2 * NTOK, :]
                step(dve.tensor_tensor(r1, r1, lam[:, 1, :].unsqueeze(1).to_broadcast([P, NTOK, HPG]), ALU.mult))
                step(dve.tensor_tensor(e, e, mx[:, :, :].unsqueeze(2).to_broadcast([P, 2 * NTOK, NTOK, HPG]),
                                       ALU.mult))
                step(dve.tensor_copy(vc[:, :, :], at[half][:, :, 4 * GW:5 * GW]))
                dve.tensor_tensor(pr[:, 0, :], pr[:, 0, :], pr[:, 1, :], ALU.subtract).then_inc(mix_ok, 1)
                dve.wait_ge(mix_ok, half + 1)

            def values(half):
                if half:
                    dve.wait_ge(oT_ps_ok, 3)

                def view(b):
                    return b.rearrange("p (n m e) -> p n e m", n=SIDE, m=NTOK)

                def products(i):
                    w, v = pv(half, i)
                    step(dve.tensor_tensor(prod.rearrange("p (n a d) -> p n a d", n=SIDE, d=DH), w, v, ALU.mult))

                products(0)
                dve.tensor_reduce(oc[:, 0:SIDE, :], view(prod), AX_X, ALU.add).then_inc(oc_ok, 1)
                dve.wait_ge(oc_ok, 2 * half + 1)
                sum_items(oc[:, SIDE:2 * SIDE, :], view)
                products(2)
                dve.tensor_reduce(oc[:, 2 * SIDE:NTOK, :], view(prod), AX_X, ALU.add).then_inc(oc_ok, 1)
                dve.wait_ge(oc_ok, 2 * half + 2)

            def attn_residual_norm(t):
                dve.wait_ge(wo_ps_ok, t + 1)
                dve.wait_ge(bo_ok, t + 1)
                dve.tensor_tensor(h0[:, t, :], h0[:, t, :], WOB[t % 2][0:TT, 0:HID], ALU.add).then_inc(h1_ok, 1)
                dve.wait_ge(h1_ok, t + 1)
                row_norm(h0[:, t, :])
                if t >= 2:
                    dve.wait_ge(tr2_ok, t - 1)
                dve.tensor_scalar(hn[:, t % 2, :], h0[:, t, :], st[:, 6:7], st[:, 18:19], ALU.subtract,
                                  ALU.mult).then_inc(hn2_ok, 1)
                dve.wait_ge(hn2_ok, t + 1)

            def ffn_residual(t):
                dve.wait_ge(pj_ok, t + 1)
                dve.wait_ge(fbadd_ok, t + 1)
                dve.tensor_tensor(h0[:, t, :], h0[:, t, :], WOB[t % 2][0:TT, 0:HID], ALU.add).then_inc(res_ok, 1)

            dve.wait_ge(ident_ok, 1)
            dve.tensor_reduce(sel[:, :], ident[:, :].rearrange("p (c b) -> p b c", b=BH), AX_X,
                              ALU.add).then_inc(sel_ok, 1)
            dve.memset(wo[:, :, :], 0.0).then_inc(zero_ok, 1)
            dve.memset(st[:, :], 1.0).then_inc(zero_ok, 1)
            dve.memset(ones[:, :], 1.0).then_inc(ones_ok, 1)
            dve.memset(whl[:, :, HID:LO].bitcast(F32), 1.0).then_inc(ones_ok, 1)
            dve.memset(xh[:, :, :, TT:XW].bitcast(F32), 1.0).then_inc(ones_ok, 1)
            dve.memset(xl[:, :, :, TT:XW].bitcast(F32), 0.0).then_inc(ones_ok, 1)
            dve.wait_ge(rows_in, 32)
            dve.tensor_copy(rows2[:, :, :].rearrange("p i (c q) -> p i q c", c=CH),
                            rows[:, :, :].rearrange("p i (q c) -> p i q c", c=CH)).then_inc(rows_ok, 1)
            dve.wait_ge(rowsT_ok, 1)
            dve.tensor_copy(gb[:, :, :].rearrange("p a b -> p (a b)"), TR[:, 0:2 * NK]).then_inc(gb_ok, 1)
            dve.wait_ge(gb_ok, 1)
            def gamma_w(k):
                dve.wait_ge(betaW_ok, k + 1)
                s = slice(k * WC, (k + 1) * WC)
                dve.tensor_tensor(wraw[:, s, :], wraw[:, s, :],
                                  gb[:, 0, s].unsqueeze(2).to_broadcast([P, WC, HID]), ALU.mult).then_inc(wg_ok, 1)

            def low_w(k):
                dve.wait_ge(wh_ok, k + 1)
                s = slice(k * WC, (k + 1) * WC)
                dve.tensor_tensor(whl[:, s, LO:YW], wraw[:, s, :], whl[:, s, 0:HID].bitcast(F32),
                                  ALU.subtract).then_inc(wl_ok, 1)

            gamma_w(0)
            turn(0, 0)
            gamma_w(1)
            low_w(0)
            turn(0, 1)
            gamma_w(2)
            turn(0, 2)
            gamma_w(3)
            turn(0, 3)
            low_w(2)
            turn(1)
            embed_norm(0)
            dve.wait_ge(small_in, 16 * 7)
            dve.wait_ge(msk_ok, 9)
            for j in range(3):
                step(dve.tensor_scalar(msk[:, :, j, :], msk[:, :, j, :], al[:, 3 + j:4 + j], None, ALU.mult))
            step(dve.tensor_tensor(cf[:, :, :], msk[:, :, 0, :], msk[:, :, 1, :], ALU.add))
            step(dve.tensor_tensor(cf[:, :, :], cf[:, :, :], msk[:, :, 2, :], ALU.add))
            for i in range(3):
                step(dve.tensor_scalar(cf[:, i, :], cf[:, i, :], al[:, i:i + 1], None, ALU.mult))
            step(dve.tensor_tensor(cf[:, 1, :], cf[:, 1, :], cf[:, 2, :], ALU.add))
            dve.tensor_tensor(cf[:, 0, :], cf[:, 0, :], cf[:, 1, :], ALU.add).then_inc(cf_ok, 1)
            step(dve.tensor_reduce(cb[:, 0:1], al[:, 3:6], AX_X, ALU.add))
            step(dve.tensor_scalar(al[:, 0:3], al[:, 0:3], cb[:, 0:1], None, ALU.mult))
            step(dve.tensor_tensor(al[:, 1:2], al[:, 1:2], al[:, 2:3], ALU.add))
            step(dve.tensor_tensor(al[:, 0:1], al[:, 0:1], al[:, 1:2], ALU.add))
            e0 = 0
            for k, e1 in enumerate(EMBED):
                dve.tensor_scalar(bc[:, 4, e0:e1], bc[:, 4, e0:e1], al[0:TT, k:k + 1], None,
                                  ALU.mult).then_inc(fb_ok, 1)
                e0 = e1
            turn(2)
            embed_norm(1)
            turn(3)
            embed_norm(2)
            turn(4)
            scores(0)
            embed_norm(3)
            turn(5)
            scores(1)
            embed_norm(4)
            scores(2)
            softmax_max(0)
            embed_norm(5)
            softmax_mix(0)
            values(0)
            scores(3)
            scores(4)
            dve.wait_ge(prep_sb, 8)
            dve.tensor_tensor(b0[:, :], b0[:, :], cf[:, 0, :], ALU.mult).then_inc(b0_ok, 1)
            scores(5)
            softmax_max(1)
            for t in range(SIDE):
                attn_residual_norm(t)
            softmax_mix(1)
            values(1)
            for t in range(SIDE):
                ffn_residual(t)
            for t in range(SIDE, TILES):
                attn_residual_norm(t)
            for t in range(SIDE, TILES):
                ffn_residual(t)

        @block.tensor
        def _(pe):
            pe.wait_ge(ident_ok, 1)
            pe.wait_ge(rows_ok, 1)
            for i in range(2):
                last = pe.transpose(TR[:, i * NK:(i + 1) * NK], rows2[:, i, :], ident[0:NK, 0:NK])
            last.then_inc(rowsT_ok, 1)
            pe.wait_ge(gb_ok, 1)
            for k in range(NK):
                if k % WC == 0:
                    pe.wait_ge(w_in[k // WC], 64)
                last = pe.matmul(PB[0:TT, 0:HID], gb[:, 1, k:k + 1].to_broadcast([P, TT]), wraw[:, k, :],
                                 start=(k == 0), stop=(k == NK - 1))
                if k % WC == WC - 1:
                    last.then_inc(betaW_ok, 1)

            def project(t, upto):
                y = Y[t % 2]
                for k in range(*upto):
                    c = NC * t + k // KC
                    if k % KC == 0:
                        pe.wait_ge(xl_ok, c + 1)
                    if k == 0 and t >= 2:
                        pe.wait_ge(y_read, t - 1)
                    if t == 0 and k % WC == 0:
                        pe.wait_ge((wl_ok, wlp_ok)[k // WC % 2], k // WC // 2 + 1)
                    if t == 0 and k == 0:
                        pe.wait_ge(ones_ok, 4)
                    pe.matmul(y[0:TT + 1, 0:YW], xh[:, k // KC, k % KC, 0:TT + 1], whl[:, k, :], start=(k == 0),
                              stop=False)
                    last = pe.matmul(y[0:TT + 1, 0:LO], xl[:, k // KC, k % KC, 0:TT + 1], whl[:, k, 0:LO],
                                     start=False, stop=(k == NK - 1))
                    if k % KC == KC - 1:
                        last.then_inc(chunk_done, 1)

            def sum_squares(t):
                pe.wait_ge(sq_ok, SIDE * (t + 1))
                pe.wait_ge(sel_ok, 1)
                for w in range(SIDE):
                    last = pe.matmul(Y[t % 2][w * BH:(w + 1) * BH, SSQ:SSQ + 1], sel[:, :],
                                     ssq[:, SIDE * t + w:SIDE * t + w + 1], start=True, stop=True)
                last.then_inc(y_ok, 1)

            def turn_rows(t):
                pe.wait_ge(hn_ok, t + 1)
                if t:
                    pe.wait_ge(hT_ok, t)
                for k in range(2):
                    last = pe.transpose(TR[0:KH, k * TT:(k + 1) * TT], hn[:, t % 2, k * KH:(k + 1) * KH],
                                        ident[0:TT, 0:TT])
                last.then_inc(tr_ok, 1)

            def heads(t):
                pe.wait_ge(hT_ok, t + 1)
                if t == 0:
                    pe.wait_ge(wqkv_in, 16 * 6)
                else:
                    pe.wait_ge(qkv_ok, t)
                w = wqkv[:, :, :].rearrange("p k (g h e) -> p k h g e", g=G5, h=HQ)
                for b in range(2):
                    for k in range(2):
                        last = pe.matmul(QK[b][0:TT, 0:2 * G5 * GW],
                                         hT[:, k, :], w[:, k, 2 * b:2 * b + 2], start=(k == 0), stop=(k == 1))
                last.then_inc(qkv_ps_ok, 1)

            project(0, (0, NK))
            sum_squares(0)
            for t in range(1, TILES):
                if t == 1:
                    project(t, (0, NK // 4))
                    pe.wait_ge(cs_ok, 1)
                    pe.matmul(PSM[0:TT, 0:HID], ones[TT:TT + 1, :], csrow, start=True, stop=True).then_inc(csb_ok, 1)
                project(t, (NK // 4 if t == 1 else 0, 3 * NK // 4))
                turn_rows(t - 1)
                project(t, (3 * NK // 4, NK))
                sum_squares(t)
                heads(t - 1)
            turn_rows(TILES - 1)
            heads(TILES - 1)
            pe.wait_ge(y_read, TILES)
            for i in range(8):
                if i >= 4:
                    pe.wait_ge(prep_sb, i - 3)
                dst = PREP[i % 4]
                if i < 4:
                    if i == 0:
                        pe.wait_ge(wsc_ok, 3)
                    ts = range(4) if i % 2 == 0 else range(4, 6)
                    for j, m in enumerate(ts):
                        last = pe.transpose(dst[0:KH, j * P:(j + 1) * P],
                                            wfc[:, m, (i // 2) * KH:(i // 2 + 1) * KH], ident[:, :])
                elif i < 7:
                    for j in range(2):
                        m = 2 * (i - 4) + j
                        for k in range(2):
                            a = j * HID + k * KH
                            last = pe.transpose(dst[:, a:a + KH], wpj[:, k, m * P:(m + 1) * P], ident[0:KH, 0:KH])
                else:
                    pe.wait_ge(small_in, 16 * 7)
                    last = pe.transpose(dst[:, 0:MT], brow[:, :], ident[0:MT, 0:MT])
                last.then_inc(prep_ps, 1)

            def post(half):
                pe.wait_ge(prep_sb, 8)
                for i in range(SIDE):
                    if i == 1:
                        pe.wait_ge(pprod_used, ITEMS * (half + 1))
                    else:
                        pe.wait_ge(oc_ok, 2 * half + (1 if i == 0 else 2))
                    for j in range(SIDE):
                        last = pe.transpose(OTB[i][0:GW, j * P:(j + 1) * P], oc[:, SIDE * i + j, :], ident[:, :])
                    last.then_inc(oT_ps_ok, 1)
                pe.wait_ge(wo_in, 16 * HQ)
                for i in range(SIDE):
                    t = SIDE * half + i
                    pe.wait_ge(oT_ok, 2 * (t + 1))
                    if i >= 2:
                        pe.wait_ge(h1_ok, t - 1)
                    if half and i < 2:
                        pe.wait_ge(res_ok, SIDE)
                    for k in range(2):
                        last = pe.matmul(WOB[t % 2][0:TT, 0:HID],
                                         oT[:, k, SIDE * i:SIDE * (i + 1), :].rearrange("p n b -> p (n b)"),
                                         wo[:, k, :], start=(k == 0), stop=(k == 1))
                    last.then_inc(wo_ps_ok, 1)
                for i in range(SIDE):
                    t = SIDE * half + i
                    pe.wait_ge(hn2_ok, t + 1)
                    if t:
                        pe.wait_ge(hT2_ok, t)
                    else:
                        pe.wait_ge(hT_ok, TILES)
                    for k in range(2):
                        last = pe.transpose(TR[0:KH, k * TT:(k + 1) * TT], hn[:, t % 2, k * KH:(k + 1) * KH],
                                            ident[0:TT, 0:TT])
                    last.then_inc(tr2_ok, 1)
                pe.wait_ge(hT2_ok, SIDE * (half + 1))
                for m in range(MT):
                    if m >= 2:
                        pe.wait_ge(gelu_ok, MT * half + m - 1)
                    elif half:
                        pe.wait_ge(gelu_ok, MT)
                    else:
                        pe.wait_ge(qkv_ok, TILES)
                    for k in range(2):
                        last = pe.matmul(QK[m % 2][:, 0:HT], w0T[:, k, m * P:(m + 1) * P], hT2[:, k, :],
                                         start=(k == 0), stop=(k == 1))
                    last.then_inc(fc_ok, 1)
                pe.wait_ge(gelu_ok, MT * (half + 1))
                pe.wait_ge(w1_ok, 3)
                for i in range(SIDE):
                    t = SIDE * half + i
                    pe.wait_ge(h1_ok, min(SIDE * (half + 1), t + 3))
                    if i >= 2:
                        pe.wait_ge(res_ok, t - 1)
                    for m in range(MT):
                        last = pe.matmul(WOB[t % 2][0:TT, 0:HID], gT[:, m, i * TT:(i + 1) * TT], w1T[:, m, :],
                                         start=(m == 0), stop=(m == MT - 1))
                    last.then_inc(pj_ok, 1)

            post(0)
            post(1)


_INS = ['x', 'L0_tok_ln1_g', 'L0_tok_ln1_b', 'L0_tok_W_proj', 'L0_tok_b_proj', 'L0_tok_ln2_g', 'L0_tok_ln2_b',
        'L0_attn_Wq', 'L0_attn_Wk', 'L0_attn_Wv', 'L0_attn_lambda_p', 'L0_attn_Wo', 'L0_attn_bo', 'L0_ffn_w_fc',
        'L0_ffn_b_fc', 'L0_ffn_w_proj', 'L0_ffn_b_proj', 'L0_ffn_alpha_e', 'L0_ffn_alpha_r']
_OUTS = [((64, 9, 192), 'float32')]


def kernel(**inputs):
    import numpy as _np
    import concourse.bacc as _bacc
    from concourse import mybir as _mybir
    from concourse.bass_utils import run_bass_kernel_spmd as _run

    nc = _bacc.Bacc("TRN2", target_bir_lowering=False, num_devices=1)
    arrays, args = {}, []
    for name in _INS:
        a = _np.ascontiguousarray(inputs[name])
        arrays[f"in_{name}_dram"] = a
        args.append(nc.dram_tensor(f"in_{name}_dram", a.shape, _mybir.dt.from_np(a.dtype), kind="ExternalInput").ap())
    for i, (shape, dtype) in enumerate(_OUTS):
        dt = _mybir.dt.from_np(_np.dtype(dtype))
        args.append(nc.dram_tensor(f"out_{i}_dram", shape, dt, kind="ExternalOutput").ap())
    vit_block(nc, *args)
    r = _run(nc, [arrays], core_ids=[0])
    got = tuple(r.results[0][f"out_{i}_dram"] for i in range(len(_OUTS)))
    return got[0]
```

```python
from contextlib import ExitStack

import concourse.bass as bass
from concourse import mybir

F32 = mybir.dt.float32
F32R = mybir.dt.float32r
ALU = mybir.AluOpType
ACT = mybir.ActivationFunctionType
AX_X = mybir.AxisListType.X

P = 128
PATCH = 32
CH = 4
D1 = CH * PATCH * PATCH
HID = 192
EPS = 1e-5
EMBED = (96, 144, 192)
RATIO = (2, 3, 4)
FF = 768


def vit_block(nc, x, ln1_g, ln1_b, W_proj, b_proj, ln2_g, ln2_b, Wq, Wk, Wv, lambda_p, Wo, bo,
              w_fc, b_fc, w_out, b_out, alpha_e, alpha_r, out):
    B, _, IMG, _ = x.shape
    SIDE = IMG // PATCH
    NTOK = SIDE * SIDE
    BH = 32
    HALVES = B // BH
    TILES = HALVES * SIDE
    TT = SIDE * BH
    HEADS = lambda_p.shape[0]
    DH = HID // HEADS
    HQ = P // BH
    HPG = HEADS // HQ
    GW = HPG * DH
    G5 = 5
    KC = 8
    NK = D1 // P
    NC = NK // KC
    SLOTS = NC
    WC = 8
    NWC = NK // WC
    YW = 2 * HID + 2
    LO = HID + 2
    KH = HID // 2
    SSQ = 400
    MT = FF // P
    HT = SIDE * TT
    SCALE = float(DH) ** -0.5
    XW = TT + 2
    PIECE = SIDE * NTOK * GW

    PIECES = [[(0, 3, 0, 3)], [(3, 3, 0, 6), (0, 3, 3, 3)], [(6, 3, 0, 9), (0, 6, 6, 3)]]
    SCORES = [[(p, m, m == 1) for p in PIECES[i] for m in range(2)] for i in range(SIDE)]
    SCORES += [[(p, m, True) for p in PIECES[0] for m in range(2)],
               [(PIECES[1][0], 0, False), (PIECES[1][0], 1, True), (PIECES[1][1], 0, True), (PIECES[1][1], 1, True)],
               [(PIECES[2][1], 0, False), (PIECES[2][0], 0, True), (PIECES[2][0], 1, True), (PIECES[2][1], 1, True)]]
    GIVEN = [sum(g for _, _, g in tile) for tile in SCORES]
    BEFORE = (sum(GIVEN[:SIDE + 1]), sum(GIVEN) + SIDE - 1)
    EARLY = sum(GIVEN[:SIDE])

    VAR, STD, RSTD, MEAN = 10, 13, 16, 20

    PARTS = [("out", 0), ("out", 1), ("out", 2), ("bias",), ("fc", 0, range(0, 4)), ("fc", 0, range(4, MT)),
             ("fc", 1, range(0, 4)), ("fc", 1, range(4, MT))]
    OUTS = 4

    ctx = ExitStack()
    with ctx:
        def sb(name, shape, dt=F32):
            return ctx.enter_context(nc.sbuf_tensor(name, shape, dt))

        def sem(name):
            return ctx.enter_context(nc.semaphore(name))

        xn = sb("xn", [P, 2, PATCH * IMG])
        xT = sb("xT", [P, SLOTS, KC * TT])
        xh = sb("xh", [P, SLOTS, KC, XW], F32R)
        xl = sb("xl", [P, SLOTS, KC, XW], F32R)
        wraw = sb("wraw", [P, NK, HID])
        whl = sb("whl", [P, NK, YW], F32R)
        squares = sb("squares", [P, PATCH * PATCH])
        oT = squares[:, 0:2 * NTOK * BH].rearrange("p (k n b) -> p k n b", k=2, n=NTOK)
        ssq = sb("ssq", [P, TILES * SIDE])
        rows = sb("rows", [NK, 2, P])
        rows2 = sb("rows2", [NK, 2, P])
        gb = sb("gb", [P, 2, NK])
        ident = sb("ident", [P, P])
        sel = sb("sel", [P, BH])
        ones = sb("ones", [P, TT])
        colsum = sb("colsum", [TT, HID])
        bias1 = sb("bias1", [TT, HID])
        bc = sb("bc", [TT, 5, HID])
        st = sb("st", [TT, 32])
        t1 = sb("t1", [TT, HID])
        t2 = sb("t2", [TT, HID])
        h0 = sb("h0", [TT, TILES, HID])
        hn = sb("hn", [TT, SIDE, HID])
        hT = sb("hT", [KH, 2, TT])
        wqkv = sb("wqkv", [KH, 2, G5 * HID])
        wo = sb("wo", [P, 2, HID])
        qkv = sb("qkv", [TT, HQ * G5 * GW])
        at = [sb(f"at{i}", [P, NTOK, G5 * GW]) for i in range(HALVES)]
        vc = sb("vc", [P, NTOK, GW])
        warm = sb("warm", [P, 2])
        pr = sb("pr", [P, 2, NTOK * NTOK * HPG])
        mx = sb("mx", [P, 2 * NTOK, HPG])
        lam = sb("lam", [P, 2, HPG])
        oc = sb("oc", [P, NTOK, GW])
        hT2 = sb("hT2", [KH, 2, HT])
        w0T = sb("w0T", [KH, 2, FF])
        w1T = sb("w1T", [P, MT, HID])
        brow = sb("brow", [MT, P])
        b0 = sb("b0", [P, MT])
        al = sb("al", [P, 6])
        msk = sb("msk", [P, 3, 3, MT])
        cf = sb("cf", [P, 3, MT])
        cb = sb("cb", [P, 3])
        flat = wraw[:, :, :].rearrange("p a b -> p (a b)")
        prod = flat[:, 0:PIECE]
        pprod = [flat[:, (1 + i) * PIECE:(2 + i) * PIECE] for i in range(2)]
        xTflat = xT[:, :, :].rearrange("p a b -> p (a b)")
        parts = whl[:, :, :].rearrange("p a b -> p (a b)")
        cut = [0]

        def part(rows, blocks, width):
            a = cut[0]
            cut[0] += blocks * width
            return parts[0:rows, a:a + blocks * width].rearrange("p (k f) -> p k f", k=blocks)

        w1p = [part(P, MT, HID) for _ in range(2)]
        gp = [part(P, MT, HT) for _ in range(2)]
        assert cut[0] <= NK * YW
        pprod += [xTflat[:, i * PIECE:(i + 1) * PIECE] for i in range(2)]
        csrow = at[1][TT:TT + 1, 0, 0:HID]
        sc0 = 3 * PIECE
        SW = 2 * NTOK * NTOK * HPG
        sc = [flat[:, sc0 + i * SW:sc0 + (i + 1) * SW].rearrange("p (a s) -> p a s", a=2) for i in range(HALVES)]
        wfc = xn[:, 0, 0:MT * HID].rearrange("p (t e) -> p t e", t=MT)
        wpj = xn[0:KH, 0, MT * HID:MT * HID + 2 * FF].rearrange("p (k h) -> p k h", k=2)
        gT = xn[:, 1, 0:MT * HT].rearrange("p (m t) -> p m t", m=MT)

        ps = ctx.enter_context(nc.psum_tensor("ps", [P, 8, 512], F32))
        Y = [ps[:, 0, :], ps[:, 1, :]]
        QK = [ps[:, 2, :], ps[:, 3, :]]
        TR = ps[:, 4, :]
        PB, PSM = ps[:, 7, :], ps[:, 6, :]
        PREP = [ps[:, 5, :], ps[:, 6, :], ps[:, 7, :]]
        OTB = [ps[:, 0, :], ps[:, 1, :], TR]
        TRB = [TR[:, 0:HID], ps[:, 0, 0:HID], ps[:, 1, 0:HID]]
        WOB = [ps[:, 5, :], ps[:, 7, :], ps[:, 6, :]]

        rows_in, w_in = sem("rows_in"), [sem(f"w_in{c}") for c in range(NWC)]
        x_in = [sem(f"x_in{i}") for i in range(2)]
        bc_in, wqkv_in, wo_in, ffn_in = sem("bc_in"), sem("wqkv_in"), sem("wo_in"), sem("ffn_in")
        small_in = sem("small_in")
        heads_out = sem("heads_out")
        at_in = [sem(f"at_in{i}") for i in range(HALVES)]
        out_done = sem("out_done")
        zeroed, ident_ok, sel_ok, ones_ok = sem("zeroed"), sem("ident_ok"), sem("sel_ok"), sem("ones_ok")
        msk_ok, zero_ok = sem("msk_ok"), sem("zero_ok")
        rows_ok, rowsT_ok, gb_ok = sem("rows_ok"), sem("rowsT_ok"), sem("gb_ok")
        betaW_ok, bias_ok = sem("betaW_ok"), sem("bias_ok")
        wg_ok, wh_ok, whd_ok, wl_ok, wlp_ok = (sem("wg_ok"), sem("wh_ok"), sem("whd_ok"), sem("wl_ok"),
                                               sem("wlp_ok"))
        cs_ok, csb_ok = sem("cs_ok"), sem("csb_ok")
        xT_ok, xh_ok, xl_ok, sq_ok = sem("xT_ok"), sem("xh_ok"), sem("xl_ok"), sem("sq_ok")
        chunk_done, y_ok, y_read = sem("chunk_done"), sem("y_ok"), sem("y_read")
        var_ok, std_ok = sem("var_ok"), sem("std_ok")
        hn_ok, tr_ok, hT_ok, qkv_ps_ok, qkv_ok = (sem("hn_ok"), sem("tr_ok"), sem("hT_ok"),
                                                  sem("qkv_ps_ok"), sem("qkv_ok"))
        pprod_ok, pprod_used = sem("pprod_ok"), sem("pprod_used")
        sc_ok, exp_ok, lam_ok, mix_ok, vc_ok = (sem("sc_ok"), sem("exp_ok"), sem("lam_ok"), sem("mix_ok"),
                                                sem("vc_ok"))
        oc_ok, oT_ps_ok, oT_ok, wo_ps_ok = sem("oc_ok"), sem("oT_ps_ok"), sem("oT_ok"), sem("wo_ps_ok")
        bo_ok, h1_ok, fbadd_ok, res_ok = sem("bo_ok"), sem("h1_ok"), sem("fbadd_ok"), sem("res_ok")
        hn2_ok, tr2_ok, hT2_ok, fc_ok, gelu_ok = (sem("hn2_ok"), sem("tr2_ok"), sem("hT2_ok"), sem("fc_ok"),
                                                  sem("gelu_ok"))
        gh_ok, gl_ok, pj_ok = sem("gh_ok"), sem("gl_ok"), sem("pj_ok")
        prep_ps, prep_sb, wsc_ok, w1_ok = sem("prep_ps"), sem("prep_sb"), sem("wsc_ok"), sem("w1_ok")
        w1h_ok, ffw_ok, b0_ok, fb_ok = sem("w1h_ok"), sem("ffw_ok"), sem("b0_ok"), sem("fb_ok")
        dve_step, act_step, pool_step = sem("dve_step"), sem("act_step"), sem("pool_step")

        heads_dram = nc.dram_tensor("heads_dram", (HALVES, HQ, BH, NTOK, G5 * GW), F32, kind="Internal").ap()

        block = ctx.enter_context(nc.Block())

        def load_x(eng, t):
            half, hrow = t // SIDE, t % SIDE
            eng.dma_start(xn[:, t % 2, :],
                          x[half * BH:(half + 1) * BH, :, hrow * PATCH:(hrow + 1) * PATCH, :]
                          .rearrange("b c p v -> c b (p v)")).then_inc(x_in[t % 2], 16)

        def load_w(eng, k):
            wv = W_proj.rearrange("(p q c) n -> c q p n", q=PATCH, c=CH)
            for c in range(CH):
                eng.dma_start(wraw[c * PATCH:(c + 1) * PATCH, k * WC:(k + 1) * WC, :],
                              wv[c, :, k * WC:(k + 1) * WC, :]).then_inc(w_in[k], 16)

        def qk(half, m, n0, nn, m0, mm):
            a, shape = at[half], [P, nn, mm, GW]
            return (a[:, n0:n0 + nn, m * GW:(m + 1) * GW].unsqueeze(2).to_broadcast(shape),
                    a[:, m0:m0 + mm, (2 + m) * GW:(3 + m) * GW].unsqueeze(1).to_broadcast(shape))

        def buffer_of(i):
            return i % 2 if i < EARLY else (i - EARLY + 2) % 4

        def last_of(i):
            return max([j for j in range(i) if buffer_of(j) == buffer_of(i)], default=-1)

        def pv(half, i):
            shape = [P, SIDE, NTOK * HPG, DH]
            return (pr[:, 0, :].rearrange("p (n a) -> p n a", n=NTOK)[:, SIDE * i:SIDE * (i + 1)].unsqueeze(3)
                    .to_broadcast(shape),
                    vc[:, :, :].rearrange("p m (h d) -> p (m h) d", d=DH).unsqueeze(1).to_broadcast(shape))

        @block.sync
        def _(sp):
            sp.dma_start(rows[:, 0, :], ln1_g.rearrange("(p k) -> p k", k=P)).then_inc(rows_in, 16)
            sp.dma_start(rows[:, 1, :], ln1_b.rearrange("(p k) -> p k", k=P)).then_inc(rows_in, 16)
            load_w(sp, 0)
            load_w(sp, 1)
            load_x(sp, 0)
            load_w(sp, 2)
            load_w(sp, 3)
            load_x(sp, 1)
            for i, v in enumerate((b_proj, ln2_g, ln2_b, bo, b_out)):
                sp.dma_start(bc[:, i, :], v.partition_broadcast(TT)).then_inc(bc_in, 16)
            for kt in range(2):
                for w, a, n in ((Wq, 0, 2 * HID), (Wk, 2 * HID, 2 * HID), (Wv, 4 * HID, HID)):
                    sp.dma_start(wqkv[:, kt, a:a + n], w[kt * KH:(kt + 1) * KH, :]).then_inc(wqkv_in, 16)
            sp.wait_ge(zero_ok, 1)
            for g in range(HQ):
                a = 64 * (g % 2)
                sp.dma_start(wo[a:a + GW, g // 2, :], Wo[g * GW:(g + 1) * GW, :]).then_inc(wo_in, 16)
            sp.dma_start(al[:, 0:3], alpha_e.partition_broadcast(P)).then_inc(small_in, 16)
            sp.dma_start(al[:, 3:6], alpha_r.partition_broadcast(P)).then_inc(small_in, 16)
            for g in range(HQ):
                sp.dma_start(lam[g * BH:(g + 1) * BH, 0, :],
                             lambda_p[g * HPG:(g + 1) * HPG, 0, 0].partition_broadcast(BH)).then_inc(small_in, 16)
            sp.dma_start(brow[:, :], b_fc.rearrange("(t p) -> t p", p=P)).then_inc(small_in, 16)

            def send_heads(t):
                half, n0 = t // SIDE, (t % SIDE) * SIDE
                sp.wait_ge(qkv_ok, t + 1)
                for w in range(SIDE):
                    sp.dma_start(heads_dram[half, :, :, n0 + w, :].rearrange("g b e -> b g e"),
                                 qkv[w * BH:(w + 1) * BH, :].rearrange("b (g e) -> b g e", g=HQ))\
                        .then_inc(heads_out, 16)
                sp.wait_ge(heads_out, 16 * SIDE * (t + 1))
                sp.dma_start(at[half][:, n0:n0 + SIDE, :],
                             heads_dram[half, :, :, n0:n0 + SIDE, :].rearrange("g b n e -> (g b) n e"))\
                    .then_inc(at_in[half], 16)

            def slot_free(t):
                sp.wait_ge(xT_ok, NC * (t + 1))
                sp.wait_ge(sq_ok, SIDE * (t + 1))

            for t in range(2, TILES):
                slot_free(t - 2)
                load_x(sp, t)
                if t >= 4:
                    send_heads(t - 4)
            slot_free(TILES - 2)
            sp.dma_start(wfc, w_fc.rearrange("(t p) e -> p t e", p=P)).then_inc(ffn_in, 16)
            sp.dma_start(wpj, w_out.rearrange("(k e) h -> e k h", k=2)).then_inc(ffn_in, 16)
            for t in range(TILES - 4, TILES):
                send_heads(t)
            for t in range(TILES):
                sp.wait_ge(res_ok, t + 1)
                half, hrow = t // SIDE, t % SIDE
                sp.dma_start(out[half * BH:(half + 1) * BH, hrow * SIDE:(hrow + 1) * SIDE, :]
                             .rearrange("b w e -> w b e"),
                             h0[:, t, :]).then_inc(out_done, 16)
            sp.wait_ge(out_done, 16 * TILES)

        @block.gpsimd
        def _(pool):
            pool.memset(ident[:, :], 0.0).then_inc(zeroed, 1)
            pool.wait_ge(zeroed, 1)
            pool.affine_select(out=ident[:, :], in_=ident[:, :], compare_op=ALU.not_equal, fill=1.0, base=0,
                               pattern=[[-1, P]], channel_multiplier=1).then_inc(ident_ok, 1)
            pool.memset(msk[:, :, :, :], 1.0).then_inc(zeroed, 1)
            pool.wait_ge(zeroed, 2)
            for i, e in enumerate(EMBED):
                for j, r in enumerate(RATIO):
                    pool.affine_select(out=msk[:, i, j, :], in_=msk[:, i, j, :], compare_op=ALU.is_gt, fill=0.0,
                                       base=r * e, pattern=[[-P, MT]], channel_multiplier=-1).then_inc(msk_ok, 1)

            def low_x(t, chunks=(0, NC)):
                with pool.Fori(*chunks) as kc:
                    pool.wait_ge(xh_ok, kc + (NC * t + 1))
                    pool.tensor_tensor(xl[:, bass.ds(kc, 1), :, 0:TT],
                                       xT[:, bass.ds(kc, 1), :].rearrange("p s (k t) -> p s k t", t=TT),
                                       xh[:, bass.ds(kc, 1), :, 0:TT].bitcast(F32), ALU.subtract).then_inc(xl_ok, 1)

            items = [0]

            def item(out, in0, in1):
                i = items[0]
                items[0] += 1
                if last_of(i) >= 0:
                    pool.wait_ge(pprod_used, last_of(i) + 1)
                pool.tensor_tensor(out(pprod[buffer_of(i)]), in0, in1, ALU.mult).then_inc(pprod_ok, 1)

            def scores(t):
                half = t // SIDE
                pool.wait_ge(at_in[half], 16 * (t % SIDE + 1))
                for (n0, nn, m0, mm), m, given in SCORES[t]:
                    if given:
                        item(lambda b: b[:, 0:nn * mm * GW].rearrange("p (n m e) -> p n m e", n=nn, m=mm),
                             *qk(half, m, n0, nn, m0, mm))

            def values(half):
                pool.wait_ge(mix_ok, half + 1)
                pool.wait_ge(vc_ok, half + 1)
                for i in range(1, SIDE):
                    item(lambda b: b.rearrange("p (n a d) -> p n a d", n=SIDE, d=DH), *pv(half, i))

            chunk = slice(WC, 2 * WC)
            gw = at[0][:, :, :].rearrange("p n e -> p (n e)")[:, 0:WC * HID].rearrange("p (k e) -> p k e", k=WC)
            pool.wait_ge(gb_ok, 1)
            pool.wait_ge(w_in[1], 16 * CH)
            pool.tensor_tensor(gw, wraw[:, chunk, :], gb[:, 0, chunk].unsqueeze(2).to_broadcast([P, WC, HID]),
                               ALU.mult).then_inc(wg_ok, 1)
            pool.wait_ge(wg_ok, 1)
            pool.wait_ge(wh_ok, 2 * WC)
            pool.tensor_tensor(whl[:, chunk, LO:YW], gw, whl[:, chunk, 0:HID].bitcast(F32),
                               ALU.subtract).then_inc(wlp_ok, 1)
            low_x(0)
            low_x(1)

            n = [0]

            def step(ins):
                n[0] += 1
                ins.then_inc(pool_step, 1)
                pool.wait_ge(pool_step, n[0])

            pool.wait_ge(small_in, 16 * 7)
            pool.wait_ge(msk_ok, 9)
            for j in range(3):
                step(pool.tensor_tensor(msk[:, :, j, :], msk[:, :, j, :],
                                        al[:, 3 + j:4 + j].unsqueeze(2).to_broadcast([P, 3, MT]), ALU.mult))
            step(pool.tensor_tensor(cf[:, :, :], msk[:, :, 0, :], msk[:, :, 1, :], ALU.add))
            step(pool.tensor_tensor(cf[:, :, :], cf[:, :, :], msk[:, :, 2, :], ALU.add))
            step(pool.tensor_tensor(cf[:, :, :], cf[:, :, :], al[:, 0:3].unsqueeze(2).to_broadcast([P, 3, MT]),
                                    ALU.mult))
            step(pool.tensor_tensor(cf[:, 1, :], cf[:, 1, :], cf[:, 2, :], ALU.add))
            step(pool.tensor_tensor(cf[:, 0, :], cf[:, 0, :], cf[:, 1, :], ALU.add))
            step(pool.tensor_tensor(cb[:, 0:1], al[:, 3:4], al[:, 4:5], ALU.add))
            step(pool.tensor_tensor(cb[:, 0:1], cb[:, 0:1], al[:, 5:6], ALU.add))
            step(pool.tensor_tensor(al[:, 0:3], al[:, 0:3], cb[:, 0:1].to_broadcast([P, 3]), ALU.mult))
            step(pool.tensor_tensor(al[:, 1:2], al[:, 1:2], al[:, 2:3], ALU.add))
            step(pool.tensor_tensor(al[:, 0:1], al[:, 0:1], al[:, 1:2], ALU.add))
            pool.wait_ge(bc_in, 16 * 5)
            e0 = 0
            for k, e1 in enumerate(EMBED):
                pool.tensor_tensor(bc[:, 4, e0:e1], bc[:, 4, e0:e1], al[0:TT, k:k + 1].to_broadcast([TT, e1 - e0]),
                                   ALU.mult).then_inc(fb_ok, 1)
                e0 = e1

            for t in range(2, TILES):
                low_x(t, (0, 2))
                if SIDE <= t < TILES - 1:
                    scores(t - SIDE)
                low_x(t, (2, NC))
            scores(SIDE - 1)
            pool.wait_ge(ffn_in, 32)
            e0 = 0
            for k, e1 in enumerate(EMBED):
                v = wfc[:, :, e0:e1]
                pool.tensor_tensor(v, v, cf[:, k, :].unsqueeze(2).to_broadcast([P, MT, e1 - e0]),
                                   ALU.mult).then_inc(wsc_ok, 1)
                e0 = e1

            def residual_bo(t):
                pool.wait_ge(hn_ok, t + 1)
                pool.tensor_tensor(h0[:, t, :], h0[:, t, :], bc[:, 3, :], ALU.add).then_inc(bo_ok, 1)

            def low_hidden(half):
                for m in range(MT - 2):
                    pool.wait_ge(gh_ok, MT * half + m + 1)
                    pool.tensor_tensor(gp[1][:, m, :], gT[:, m, :], gp[0][:, m, :].bitcast(F32),
                                       ALU.subtract).then_inc(gl_ok, 1)

            def residual_fb(t):
                pool.wait_ge(fb_ok, 3)
                pool.wait_ge(hn2_ok, t + 1)
                pool.tensor_tensor(h0[:, t, :], h0[:, t, :], bc[:, 4, :], ALU.add).then_inc(fbadd_ok, 1)

            for t in range(SIDE):
                residual_bo(t)
            pool.wait_ge(prep_sb, 3)
            e0 = 0
            for k, e1 in enumerate(EMBED):
                v = w1T[:, :, e0:e1]
                pool.tensor_tensor(v, v, cf[:, k, :].unsqueeze(2).to_broadcast([P, MT, e1 - e0]),
                                   ALU.mult).then_inc(w1_ok, 1)
                e0 = e1
            pool.wait_ge(xl_ok, NC * TILES)
            scores(3)
            pool.wait_ge(w1h_ok, 1)
            pool.tensor_tensor(w1p[1], w1T[:, :, :], w1p[0].bitcast(F32), ALU.subtract).then_inc(ffw_ok, 1)
            pool.wait_ge(prep_sb, OUTS)
            pool.tensor_tensor(b0[:, :], b0[:, :], cf[:, 0, :], ALU.mult).then_inc(b0_ok, 1)
            values(0)
            scores(4)
            scores(5)
            for t in range(SIDE, TILES):
                residual_bo(t)
            for t in range(SIDE):
                residual_fb(t)
            low_hidden(0)
            values(1)
            for t in range(SIDE, TILES):
                residual_fb(t)

        @block.scalar
        def _(act):
            lns = [0]

            def sqrt_(tiles=1):
                lns[0] += 1
                act.wait_ge(var_ok, lns[0])
                act.activation(st[:, STD:STD + tiles], st[:, VAR:VAR + tiles], ACT.Sqrt).then_inc(std_ok, 1)

            def split_high(t, chunks=(0, NC)):
                for kc in range(*chunks):
                    act.wait_ge(xT_ok, NC * t + kc + 1)
                    if t:
                        act.wait_ge(chunk_done, NC * (t - 1) + kc + 1)
                    act.activation(xh[:, kc, :, 0:TT], xT[:, kc, :].rearrange("p (k t) -> p k t", t=TT),
                                   ACT.Copy).then_inc(xh_ok, 1)

            def square(t, *ws):
                act.wait_ge(x_in[t % 2], 16 * (t // 2 + 1))
                v = xn[:, t % 2, :].rearrange("p (r w q) -> p w r q", w=SIDE, q=PATCH)
                for w in ws or range(SIDE):
                    if SIDE * t + w:
                        act.wait_ge(sq_ok, SIDE * t + w)
                    act.activation(squares.rearrange("p (r q) -> p r q", q=PATCH), v[:, w], ACT.Square,
                                   accum_out=ssq[:, SIDE * t + w:SIDE * t + w + 1]).then_inc(sq_ok, 1)

            def hT_copy(t):
                act.wait_ge(tr_ok, t + 1)
                act.activation(hT[:, :, :].rearrange("p k t -> p (k t)"), TR[0:KH, 0:2 * TT],
                               ACT.Copy).then_inc(hT_ok, 1)

            def qkv_copy(t):
                act.wait_ge(qkv_ps_ok, t + 1)
                if t:
                    act.wait_ge(heads_out, 16 * SIDE * t)
                w = 2 * G5 * GW
                act.activation(qkv[:, 0:w], QK[0][0:TT, 0:w], ACT.Copy).then_inc(act_step, 1)
                act.activation(qkv[:, w:2 * w], QK[1][0:TT, 0:w], ACT.Copy).then_inc(qkv_ok, 1)

            def high_w(c):
                act.wait_ge(w_in[c], 16 * CH)
                for k in range(c * WC, (c + 1) * WC):
                    act.activation(whl[:, k, 0:HID], wraw[:, k, :], ACT.Copy,
                                   scale=gb[:, 0, k:k + 1]).then_inc(wh_ok, 1)

            def table(func):
                act.activation(warm[0:1, 1:2], warm[0:1, 0:1], func).then_inc(act_step, 1)

            def gather_values(half):
                act.wait_ge(at_in[half], 16 * SIDE)
                if half:
                    act.wait_ge(oc_ok, 1)
                    act.wait_ge(pprod_used, BEFORE[0] + SIDE - 1)
                act.activation(vc[:, :, :], at[half][:, :, 4 * GW:5 * GW], ACT.Copy).then_inc(vc_ok, 1)

            def exp_(half):
                act.wait_ge(sc_ok, half + 1)
                act.activation(pr[:, :, :].rearrange("p a b -> p (a b)"), sc[half].rearrange("p a b -> p (a b)"),
                               ACT.Exp, scale=SCALE).then_inc(exp_ok, 1)

            def ffn_weights(some):
                for i in some:
                    part = PARTS[i]
                    act.wait_ge(prep_ps, i + 1)
                    src = PREP[i % 3]
                    if part[0] == "out":
                        a = 2 * part[1]
                        act.activation(w1T[:, a:a + 2, :].rearrange("p t e -> p (t e)"), src[:, 0:2 * HID],
                                       ACT.Copy).then_inc(prep_sb, 1)
                    elif part[0] == "bias":
                        act.activation(b0[:, :], src[:, 0:MT], ACT.Copy).then_inc(prep_sb, 1)
                    else:
                        a, n = part[2][0] * P, len(part[2]) * P
                        act.activation(w0T[:, part[1], a:a + n], src[0:KH, 0:n], ACT.Copy).then_inc(prep_sb, 1)

            act.wait_ge(zero_ok, 2)
            table(ACT.Sqrt)
            act.wait_ge(gb_ok, 1)
            high_w(0)
            high_w(1)
            split_high(0, (0, 2))
            high_w(2)
            split_high(0, (2, NC))
            square(0)
            split_high(1)
            for t in range(TILES):
                ahead = t + 2 if t else 1
                for i in range(SIDE):
                    sqrt_()
                    if ahead < TILES:
                        square(ahead, i)
                    if t == TILES - 1 and i == 1:
                        ffn_weights(range(OUTS))
                if t:
                    qkv_copy(t - 1)
                if t + 2 < TILES:
                    split_high(t + 2, (0, 2))
                hT_copy(t)
                if t + 2 < TILES:
                    split_high(t + 2, (2, NC))
                if t == 0:
                    square(2)
            act.wait_ge(w1_ok, 3)
            act.wait_ge(chunk_done, NC * TILES)
            act.activation(w1p[0], w1T[:, :, :], ACT.Copy).then_inc(w1h_ok, 1)
            act.wait_ge(small_in, 16 * 7)
            act.activation(lam[:, 1, :], lam[:, 0, :], ACT.Exp).then_inc(lam_ok, 1)
            gather_values(0)
            exp_(0)
            qkv_copy(TILES - 1)
            ffn_weights(range(OUTS, len(PARTS)))
            table(ACT.Sqrt)

            def attention_out(half):
                for i in range(SIDE):
                    act.wait_ge(oT_ps_ok, SIDE * half + i + 1)
                    src = OTB[i][0:GW, 0:SIDE * P].rearrange("p (n k g b) -> p g k n b", k=2, g=2, b=BH)
                    for g in range(2):
                        act.activation(oT[64 * g:64 * g + GW, :, SIDE * i:SIDE * (i + 1), :], src[:, g],
                                       ACT.Copy).then_inc(oT_ok, 1)
                if half == 0:
                    gather_values(1)
                sqrt_(SIDE)
                table(ACT.Gelu_apprx_tanh)
                for i in range(SIDE):
                    act.wait_ge(tr2_ok, SIDE * half + i + 1)
                    act.activation(hT2[:, :, i * TT:(i + 1) * TT],
                                   TRB[i][0:KH, :].rearrange("p (k t) -> p k t", k=2),
                                   ACT.Copy).then_inc(hT2_ok, 1)

            def hidden(half, *ms):
                act.wait_ge(b0_ok, 1)
                for m in ms:
                    act.wait_ge(fc_ok, MT * half + m + 1)
                    if half:
                        act.wait_ge(pj_ok, SIDE)
                    act.activation(gT[:, m, :], QK[m % 2][:, 0:HT], ACT.Gelu_apprx_tanh,
                                   bias=b0[:, m:m + 1]).then_inc(gelu_ok, 1)
                    act.wait_ge(gelu_ok, MT * half + m + 1)
                    act.activation(gp[0][:, m, :], gT[:, m, :], ACT.Copy).then_inc(gh_ok, 1)

            attention_out(0)
            hidden(0, 0, 1)
            table(ACT.Exp)
            exp_(1)
            hidden(0, 2, 3, 4, 5)
            table(ACT.Sqrt)
            attention_out(1)
            hidden(1, *range(MT))

        @block.vector
        def _(dve):
            n = [0]

            def step(ins):
                n[0] += 1
                ins.then_inc(dve_step, 1)
                dve.wait_ge(dve_step, n[0])

            lns = [0]

            def rstd(tiles=1):
                lns[0] += 1
                dve.wait_ge(std_ok, lns[0])
                step(dve.reciprocal(st[:, RSTD:RSTD + tiles], st[:, STD:STD + tiles]))

            def turn(t, *kcs):
                dve.wait_ge(x_in[t % 2], 16 * (t // 2 + 1))
                for kc in kcs or range(NC):
                    c = NC * t + kc
                    if c >= SLOTS:
                        dve.wait_ge(xl_ok, c - SLOTS + 1)
                    w = KC * TT
                    dve.transpose(xT[:, kc, :], xn[:, t % 2, kc * w:(kc + 1) * w]).then_inc(xT_ok, 1)

            def variance(src):
                step(dve.bn_stats(st[:, 0:6], src))
                step(dve.bn_aggr(st[:, MEAN:MEAN + 2], st[:, 0:6]))
                dve.tensor_scalar(st[:, VAR:VAR + 1], st[:, MEAN + 1:MEAN + 2], EPS, None, ALU.add).then_inc(var_ok, 1)


            def patch_variance(t):
                y = Y[t % 2]
                dve.wait_ge(y_ok, t + 1)
                if t == 0:
                    step(dve.tensor_copy(csrow, y[TT:TT + 1, 0:HID]))
                    dve.tensor_tensor(csrow, csrow, y[TT:TT + 1, LO:YW], ALU.add).then_inc(cs_ok, 1)
                    dve.wait_ge(csb_ok, 1)
                    step(dve.tensor_copy(colsum[:, :], PSM[0:TT, 0:HID]))
                step(dve.tensor_scalar(st[:, 8:9], y[0:TT, HID:HID + 1], -1.0 / D1, None, ALU.mult))
                step(dve.tensor_scalar(st[:, 9:10], st[:, 8:9], st[:, 8:9], EPS, ALU.mult, ALU.subtract))
                dve.scalar_tensor_tensor(out=st[:, VAR:VAR + 1], in0=y[0:TT, SSQ:SSQ + 1], scalar=1.0 / D1,
                                         in1=st[:, 9:10], op0=ALU.mult, op1=ALU.subtract).then_inc(var_ok, 1)
                step(dve.scalar_tensor_tensor(out=t1[:, :], in0=colsum[:, :], scalar=st[:, 8:9],
                                              in1=y[0:TT, 0:HID], op0=ALU.mult, op1=ALU.add))
                dve.tensor_tensor(t2[:, :], t1[:, :], y[0:TT, LO:YW], ALU.add).then_inc(y_read, 1)
                if t == 0:
                    dve.wait_ge(bc_in, 16 * 5)
                    dve.wait_ge(betaW_ok, NWC)
                    dve.tensor_tensor(bias1[:, :], bc[:, 0, :], PB[0:TT, 0:HID], ALU.add).then_inc(bias_ok, 1)
                    dve.wait_ge(bias_ok, 1)

            def project_rows(t):
                rstd()
                dve.wait_ge(y_read, t + 1)
                step(dve.scalar_tensor_tensor(out=t1[:, :], in0=t2[:, :], scalar=st[:, RSTD:RSTD + 1],
                                              in1=bias1[:, :], op0=ALU.mult, op1=ALU.add))
                variance(t1[:, :])

            def embed_rows(t):
                rstd()
                step(dve.tensor_scalar(t2[:, :], t1[:, :], st[:, MEAN:MEAN + 1], st[:, RSTD:RSTD + 1],
                                       ALU.subtract, ALU.mult))
                step(dve.tensor_tensor(t1[:, :], t2[:, :], bc[:, 1, :], ALU.mult))
                step(dve.tensor_tensor(h0[:, t, :], t1[:, :], bc[:, 2, :], ALU.add))
                variance(h0[:, t, :])

            def norm_rows(t):
                rstd()
                if t >= SIDE:
                    dve.wait_ge(tr_ok, t - SIDE + 1)
                dve.tensor_scalar(hn[:, t % SIDE, :], h0[:, t, :], st[:, MEAN:MEAN + 1], st[:, RSTD:RSTD + 1],
                                  ALU.subtract, ALU.mult).then_inc(hn_ok, 1)

            used = [0]

            def sum_items(out, view):
                used[0] += 1
                dve.wait_ge(pprod_ok, used[0])
                dve.tensor_reduce(out, view(pprod[buffer_of(used[0] - 1)]), AX_X, ALU.add).then_inc(pprod_used, 1)
                dve.wait_ge(pprod_used, used[0])

            def scores(t, some=slice(None)):
                half = t // SIDE
                dve.wait_ge(at_in[half], 16 * (t % SIDE + 1))
                for (n0, nn, m0, mm), m, given in SCORES[t][some]:
                    def view(b):
                        return b[:, 0:nn * mm * GW].rearrange("p (n a d) -> p n a d", n=nn, d=DH)

                    out = sc[half][:, m, :].rearrange("p (n a) -> p n a", n=NTOK)[:, n0:n0 + nn,
                                                                                  m0 * HPG:(m0 + mm) * HPG]
                    if given:
                        sum_items(out, view)
                    else:
                        q, k = qk(half, m, n0, nn, m0, mm)
                        step(dve.tensor_tensor(prod[:, 0:nn * mm * GW].rearrange("p (n m e) -> p n m e", n=nn, m=mm),
                                               q, k, ALU.mult))
                        step(dve.tensor_reduce(out, view(prod), AX_X, ALU.add))

            def by_row(v):
                return v.rearrange("p a (n m h) -> p (a n) m h", n=NTOK, m=NTOK)

            def softmax_max(half):
                s = by_row(sc[half])
                step(dve.tensor_reduce(mx[:, :, :], s.rearrange("p a m h -> p a h m"), AX_X, ALU.max))
                dve.tensor_tensor(s, s, mx[:, :, :].unsqueeze(2).to_broadcast([P, 2 * NTOK, NTOK, HPG]),
                                  ALU.subtract).then_inc(sc_ok, 1)

            def softmax_mix(half):
                e = by_row(pr[:, :, :])
                dve.wait_ge(exp_ok, half + 1)
                step(dve.tensor_reduce(mx[:, :, :], e.rearrange("p a m h -> p a h m"), AX_X, ALU.add))
                step(dve.reciprocal(mx[:, :, :], mx[:, :, :]))
                dve.wait_ge(lam_ok, 1)
                r1 = mx[:, NTOK:2 * NTOK, :]
                step(dve.tensor_tensor(r1, r1, lam[:, 1, :].unsqueeze(1).to_broadcast([P, NTOK, HPG]), ALU.mult))
                step(dve.tensor_tensor(e, e, mx[:, :, :].unsqueeze(2).to_broadcast([P, 2 * NTOK, NTOK, HPG]),
                                       ALU.mult))
                dve.tensor_tensor(pr[:, 0, :], pr[:, 0, :], pr[:, 1, :], ALU.subtract).then_inc(mix_ok, 1)
                dve.wait_ge(mix_ok, half + 1)

            def values(half):
                if half:
                    dve.wait_ge(oT_ps_ok, 3)

                def view(b):
                    return b.rearrange("p (n m e) -> p n e m", n=SIDE, m=NTOK)

                dve.wait_ge(vc_ok, half + 1)
                w, v = pv(half, 0)
                step(dve.tensor_tensor(prod.rearrange("p (n a d) -> p n a d", n=SIDE, d=DH), w, v, ALU.mult))
                dve.tensor_reduce(oc[:, 0:SIDE, :], view(prod), AX_X, ALU.add).then_inc(oc_ok, 1)
                dve.wait_ge(oc_ok, half + 1)
                if half:
                    low_hidden(0, MT - 2, MT - 1)
                    for t in range(SIDE):
                        ffn_residual(t)
                for i in range(1, SIDE):
                    sum_items(oc[:, SIDE * i:SIDE * (i + 1), :], view)

            def attn_residual_norm(half):
                for i in range(SIDE):
                    t = SIDE * half + i
                    dve.wait_ge(wo_ps_ok, t + 1)
                    dve.wait_ge(bo_ok, t + 1)
                    dve.tensor_tensor(h0[:, t, :], h0[:, t, :], WOB[i][0:TT, 0:HID], ALU.add).then_inc(h1_ok, 1)
                    dve.wait_ge(h1_ok, t + 1)
                    step(dve.bn_stats(st[:, 0:6], h0[:, t, :]))
                    step(dve.bn_aggr(st[:, MEAN + 2 * i:MEAN + 2 * i + 2], st[:, 0:6]))
                mv = st[:, MEAN:MEAN + 2 * SIDE].rearrange("p (i s) -> p s i", s=2)
                dve.tensor_scalar(st[:, VAR:VAR + SIDE], mv[:, 1, :], EPS, None, ALU.add).then_inc(var_ok, 1)
                rstd(SIDE)
                for i in range(SIDE):
                    t = SIDE * half + i
                    dve.tensor_scalar(hn[:, i, :], h0[:, t, :], mv[:, 0, i:i + 1], st[:, RSTD + i:RSTD + i + 1],
                                      ALU.subtract, ALU.mult).then_inc(hn2_ok, 1)

            def low_hidden(half, *ms):
                for m in ms:
                    dve.wait_ge(gh_ok, MT * half + m + 1)
                    if half == 0:
                        dve.wait_ge(gl_ok, m)
                    dve.tensor_tensor(gp[1][:, m, :], gT[:, m, :], gp[0][:, m, :].bitcast(F32),
                                      ALU.subtract).then_inc(gl_ok, 1)

            def ffn_residual(t):
                dve.wait_ge(pj_ok, t + 1)
                dve.wait_ge(fbadd_ok, t + 1)
                dve.tensor_tensor(h0[:, t, :], h0[:, t, :], WOB[t % SIDE][0:TT, 0:HID], ALU.add).then_inc(res_ok, 1)

            dve.wait_ge(ident_ok, 1)
            dve.tensor_reduce(sel[:, :], ident[:, :].rearrange("p (c b) -> p b c", b=BH), AX_X,
                              ALU.add).then_inc(sel_ok, 1)
            dve.memset(wo[:, :, :], 0.0).then_inc(zero_ok, 1)
            dve.memset(warm[:, :], 1.0).then_inc(zero_ok, 1)
            dve.memset(ones[:, :], 1.0).then_inc(ones_ok, 1)
            dve.memset(whl[:, :, HID:LO].bitcast(F32), 1.0).then_inc(ones_ok, 1)
            dve.memset(xh[:, :, :, TT:XW].bitcast(F32), 1.0).then_inc(ones_ok, 1)
            dve.memset(xl[:, :, :, TT:XW].bitcast(F32), 0.0).then_inc(ones_ok, 1)
            dve.wait_ge(rows_in, 32)
            dve.tensor_copy(rows2[:, :, :].rearrange("p i (c q) -> p i q c", c=CH),
                            rows[:, :, :].rearrange("p i (q c) -> p i q c", c=CH)).then_inc(rows_ok, 1)
            dve.wait_ge(rowsT_ok, 1)
            dve.tensor_copy(gb[:, :, :].rearrange("p a b -> p (a b)"), TR[:, 0:2 * NK]).then_inc(gb_ok, 1)
            dve.wait_ge(gb_ok, 1)

            def low_w(c):
                for k in range(c * WC, (c + 1) * WC):
                    if c < NWC - 1:
                        dve.wait_ge(wh_ok, k + 1)
                    dve.scalar_tensor_tensor(out=whl[:, k, LO:YW], in0=wraw[:, k, :], scalar=gb[:, 0, k:k + 1],
                                             in1=whl[:, k, 0:HID].bitcast(F32), op0=ALU.mult,
                                             op1=ALU.subtract).then_inc(wl_ok, 1)

            def high_w(c):
                for k in range(c * WC, (c + 1) * WC):
                    dve.tensor_scalar(whl[:, k, 0:HID], wraw[:, k, :], gb[:, 0, k:k + 1], None,
                                      ALU.mult).then_inc(whd_ok, 1)
                dve.wait_ge(whd_ok, WC)

            low_w(0)
            turn(0, 0)
            turn(0, 1)
            turn(0, 2)
            low_w(2)
            turn(0, 3)
            dve.wait_ge(w_in[3], 16 * CH)
            high_w(3)
            low_w(3)
            turn(1)
            for t in range(2):
                patch_variance(t)
                project_rows(t)
                embed_rows(t)
                norm_rows(t)
                turn(t + 2)
            patch_variance(2)
            project_rows(2)
            turn(4, 0)
            embed_rows(2)
            turn(4, 1)
            norm_rows(2)
            turn(4, 2, 3)
            scores(0)
            patch_variance(3)
            project_rows(3)
            turn(5, 0)
            embed_rows(3)
            turn(5, 1)
            norm_rows(3)
            turn(5, 2, 3)
            scores(1, slice(0, 2))
            patch_variance(4)
            project_rows(4)
            scores(1, slice(2, 3))
            embed_rows(4)
            scores(1, slice(3, 4))
            norm_rows(4)
            scores(2, slice(0, 1))
            patch_variance(5)
            project_rows(5)
            embed_rows(5)
            norm_rows(5)
            scores(2, slice(1, None))
            softmax_max(0)
            scores(3)
            softmax_mix(0)
            values(0)
            scores(4)
            attn_residual_norm(0)
            scores(5)
            softmax_max(1)
            softmax_mix(1)
            values(1)
            attn_residual_norm(1)
            low_hidden(1, *range(MT))
            for t in range(SIDE, TILES):
                ffn_residual(t)

        @block.tensor
        def _(pe):
            pe.wait_ge(ident_ok, 1)
            pe.wait_ge(rows_ok, 1)
            for i in range(2):
                last = pe.transpose(TR[:, i * NK:(i + 1) * NK], rows2[:, i, :], ident[0:NK, 0:NK])
            last.then_inc(rowsT_ok, 1)
            pe.wait_ge(gb_ok, 1)

            def beta_w(c):
                pe.wait_ge(w_in[c], 16 * CH)
                for k in range(c * WC, (c + 1) * WC):
                    last = pe.matmul(PB[0:TT, 0:HID], gb[:, 1, k:k + 1].to_broadcast([P, TT]), wraw[:, k, :],
                                     start=(k == 0), stop=(k == NK - 1))
                last.then_inc(betaW_ok, 1)

            def project(t, upto):
                y = Y[t % 2]
                for k in range(*upto):
                    c = NC * t + k // KC
                    if k % KC == 0:
                        pe.wait_ge(xl_ok, c + 1)
                    if k == 0 and t >= 2:
                        pe.wait_ge(y_read, t - 1)
                    if t == 0 and k % WC == 0:
                        if k == WC:
                            pe.wait_ge(wlp_ok, 1)
                        else:
                            pe.wait_ge(wl_ok, WC if k == 0 else k)
                    if t == 0 and k == 0:
                        pe.wait_ge(ones_ok, 4)
                    pe.matmul(y[0:TT + 1, 0:YW], xh[:, k // KC, k % KC, 0:TT + 1], whl[:, k, :], start=(k == 0),
                              stop=False)
                    last = pe.matmul(y[0:TT + 1, 0:LO], xl[:, k // KC, k % KC, 0:TT + 1], whl[:, k, 0:LO],
                                     start=False, stop=(k == NK - 1))
                    if k % KC == KC - 1:
                        last.then_inc(chunk_done, 1)

            def sum_squares(t):
                pe.wait_ge(sq_ok, SIDE * (t + 1))
                pe.wait_ge(sel_ok, 1)
                for w in range(SIDE):
                    last = pe.matmul(Y[t % 2][w * BH:(w + 1) * BH, SSQ:SSQ + 1], sel[:, :],
                                     ssq[:, SIDE * t + w:SIDE * t + w + 1], start=True, stop=True)
                last.then_inc(y_ok, 1)

            def turn_rows(t):
                pe.wait_ge(hn_ok, t + 1)
                if t:
                    pe.wait_ge(hT_ok, t)
                for k in range(2):
                    last = pe.transpose(TR[0:KH, k * TT:(k + 1) * TT], hn[:, t % SIDE, k * KH:(k + 1) * KH],
                                        ident[0:TT, 0:TT])
                last.then_inc(tr_ok, 1)

            def heads(t):
                pe.wait_ge(hT_ok, t + 1)
                if t == 0:
                    pe.wait_ge(wqkv_in, 16 * 6)
                else:
                    pe.wait_ge(qkv_ok, t)
                w = wqkv[:, :, :].rearrange("p k (g h e) -> p k h g e", g=G5, h=HQ)
                for b in range(2):
                    for k in range(2):
                        last = pe.matmul(QK[b][0:TT, 0:2 * G5 * GW],
                                         hT[:, k, :], w[:, k, 2 * b:2 * b + 2], start=(k == 0), stop=(k == 1))
                last.then_inc(qkv_ps_ok, 1)

            def ffn_weights(some):
                for i in some:
                    part = PARTS[i]
                    if i >= 3:
                        pe.wait_ge(prep_sb, i - 2)
                    dst = PREP[i % 3]
                    if part[0] == "out":
                        for j in range(2):
                            m = 2 * part[1] + j
                            for k in range(2):
                                a = j * HID + k * KH
                                last = pe.transpose(dst[:, a:a + KH], wpj[:, k, m * P:(m + 1) * P],
                                                    ident[0:KH, 0:KH])
                    elif part[0] == "bias":
                        last = pe.transpose(dst[:, 0:MT], brow[:, :], ident[0:MT, 0:MT])
                    else:
                        pe.wait_ge(wsc_ok, 3)
                        for j, m in enumerate(part[2]):
                            last = pe.transpose(dst[0:KH, j * P:(j + 1) * P],
                                                wfc[:, m, part[1] * KH:(part[1] + 1) * KH], ident[:, :])
                    last.then_inc(prep_ps, 1)

            beta_w(0)
            beta_w(1)
            beta_w(2)
            project(0, (0, NK))
            sum_squares(0)
            pe.wait_ge(cs_ok, 1)
            pe.matmul(PSM[0:TT, 0:HID], ones[TT:TT + 1, :], csrow, start=True, stop=True).then_inc(csb_ok, 1)
            beta_w(3)
            for t in range(1, TILES):
                project(t, (0, 3 * NK // 4))
                if t > 1:
                    turn_rows(t - 1)
                project(t, (3 * NK // 4, NK))
                sum_squares(t)
                if t == 1:
                    turn_rows(0)
                heads(t - 1)
            pe.wait_ge(small_in, 16 * 7)
            pe.wait_ge(ffn_in, 32)
            ffn_weights(range(OUTS))
            turn_rows(TILES - 1)
            heads(TILES - 1)
            ffn_weights(range(OUTS, len(PARTS)))
            def post(half):
                pe.wait_ge(prep_sb, 8)
                def turn_output(i):
                    if i == 0:
                        pe.wait_ge(oc_ok, half + 1)
                    else:
                        pe.wait_ge(pprod_used, BEFORE[half] + i)
                    for j in range(SIDE):
                        last = pe.transpose(OTB[i][0:GW, j * P:(j + 1) * P], oc[:, SIDE * i + j, :], ident[:, :])
                    last.then_inc(oT_ps_ok, 1)

                def output(i):
                    t = SIDE * half + i
                    pe.wait_ge(oT_ok, 2 * (t + 1))
                    if half:
                        pe.wait_ge(res_ok, i + 1)
                    for k in range(2):
                        last = pe.matmul(WOB[i][0:TT, 0:HID],
                                         oT[:, k, SIDE * i:SIDE * (i + 1), :].rearrange("p n b -> p (n b)"),
                                         wo[:, k, :], start=(k == 0), stop=(k == 1))
                    last.then_inc(wo_ps_ok, 1)

                pe.wait_ge(wo_in, 16 * HQ)
                turn_output(0)
                turn_output(1)
                output(0)
                turn_output(2)
                output(1)
                output(2)
                pe.wait_ge(oT_ok, 2 * SIDE * (half + 1))
                if half == 0:
                    pe.wait_ge(hT_ok, TILES)
                for i in range(SIDE):
                    pe.wait_ge(hn2_ok, SIDE * half + i + 1)
                    for k in range(2):
                        last = pe.transpose(TRB[i][0:KH, k * TT:(k + 1) * TT], hn[:, i, k * KH:(k + 1) * KH],
                                            ident[0:TT, 0:TT])
                    last.then_inc(tr2_ok, 1)
                both = ((0, 0), (0, 1), (1, 0))
                pe.wait_ge(hT2_ok, SIDE * (half + 1))
                pe.wait_ge(ffw_ok, 1)
                if half == 0:
                    pe.wait_ge(qkv_ok, TILES)

                def first(m):
                    if MT * half + m >= 2:
                        pe.wait_ge(gelu_ok, MT * half + m - 1)
                    for k in range(2):
                        last = pe.matmul(QK[m % 2][:, 0:HT], w0T[:, k, m * P:(m + 1) * P], hT2[:, k, :],
                                         start=(k == 0), stop=(k == 1))
                    last.then_inc(fc_ok, 1)

                pe.wait_ge(h1_ok, SIDE * (half + 1))
                first(0)
                first(1)
                for m in range(MT):
                    if m + 2 < MT:
                        first(m + 2)
                    pe.wait_ge(gl_ok, MT * half + m + 1)
                    for i in range(SIDE):
                        for a, b in both:
                            last = pe.matmul(WOB[i][0:TT, 0:HID], gp[a][:, m, i * TT:(i + 1) * TT], w1p[b][:, m, :],
                                             start=(m == 0 and a + b == 0), stop=(m == MT - 1 and a == 1))
                        if m == MT - 1:
                            last.then_inc(pj_ok, 1)

            post(0)
            post(1)


_INS = ['x', 'L0_tok_ln1_g', 'L0_tok_ln1_b', 'L0_tok_W_proj', 'L0_tok_b_proj', 'L0_tok_ln2_g', 'L0_tok_ln2_b',
        'L0_attn_Wq', 'L0_attn_Wk', 'L0_attn_Wv', 'L0_attn_lambda_p', 'L0_attn_Wo', 'L0_attn_bo', 'L0_ffn_w_fc',
        'L0_ffn_b_fc', 'L0_ffn_w_proj', 'L0_ffn_b_proj', 'L0_ffn_alpha_e', 'L0_ffn_alpha_r']
_OUTS = [((64, 9, 192), 'float32')]


def kernel(**inputs):
    import numpy as _np
    import concourse.bacc as _bacc
    from concourse import mybir as _mybir
    from concourse.bass_utils import run_bass_kernel_spmd as _run

    nc = _bacc.Bacc("TRN2", target_bir_lowering=False, num_devices=1)
    arrays, args = {}, []
    for name in _INS:
        a = _np.ascontiguousarray(inputs[name])
        arrays[f"in_{name}_dram"] = a
        args.append(nc.dram_tensor(f"in_{name}_dram", a.shape, _mybir.dt.from_np(a.dtype), kind="ExternalInput").ap())
    for i, (shape, dtype) in enumerate(_OUTS):
        dt = _mybir.dt.from_np(_np.dtype(dtype))
        args.append(nc.dram_tensor(f"out_{i}_dram", shape, dt, kind="ExternalOutput").ap())
    vit_block(nc, *args)
    r = _run(nc, [arrays], core_ids=[0])
    got = tuple(r.results[0][f"out_{i}_dram"] for i in range(len(_OUTS)))
    return got[0]
```
